# Optimizing a Trainium2 kernel written in Bass

```python
import numpy as np
import jax
import jax.numpy as jnp

def _softmax(x, axis=-1):
    return jax.nn.softmax(x, axis=axis)

def _gelu(x):
    return jax.nn.gelu(x, approximate=True)

def _silu(x):
    return jax.nn.silu(x)

def _sigmoid(x):
    return jax.nn.sigmoid(x)

def _layernorm(x, axis=-1, eps=1e-05):
    m = jnp.mean(x, axis=axis, keepdims=True)
    v = jnp.var(x, axis=axis, keepdims=True)
    return (x - m) / jnp.sqrt(v + eps)

def _scatter_add(tgt, idx, src, axis=0):
    return tgt.at[idx].add(src)

def _segment_sum(src, seg, n):
    return jax.ops.segment_sum(src, seg, n)
kernel_name = 'mk_vit_tower_d1_tok_img768_r4_a8e94f'

def setup_inputs(seed: int=0):
    np.random.seed(seed)
    _w = jnp.asarray

    def _rec_inputs():
        import jax
        import jax.numpy as jnp
        _rk = jax.random.key(seed)
        x = 7.57192e-06 + 1.00007 * jax.random.normal(jax.random.fold_in(_rk, 1), (32, 128, 128, 3), jnp.float32)
        return x
    x = _rec_inputs()

    def _L0_tok_setup():
        import jax, jax.numpy as jnp
        import numpy as np
        PATCH = 16
        DIM = 192
        EPS = 0.001

        def _shifts(x):
            zw = jnp.zeros_like(x[:, :, :1, :])
            right = jnp.concatenate([zw, x[:, :, :-1, :]], axis=2)
            left = jnp.concatenate([x[:, :, 1:, :], zw], axis=2)
            zh = jnp.zeros_like(x[:, :1, :, :])
            down = jnp.concatenate([zh, x[:, :-1, :, :]], axis=1)
            up = jnp.concatenate([x[:, 1:, :, :], zh], axis=1)
            return [right, left, down, up]

        def _patchify(x, p):
            b, H, W, C = x.shape
            hh, ww = (H // p, W // p)
            x = x.reshape(b, hh, p, ww, p, C)
            x = x.transpose(0, 1, 3, 2, 4, 5)
            return x.reshape(b, hh * ww, p * p * C)
        key = jax.random.key(seed)
        k1, k2 = jax.random.split(key)
        b, H, Wd, C = (64, 224, 224, 3)
        F = PATCH * PATCH * 5 * C
        x = jax.random.normal(k1, (b, H, Wd, C), dtype=jnp.float32)
        gamma = jnp.ones((F,), dtype=jnp.float32)
        beta = jnp.zeros((F,), dtype=jnp.float32)
        W = jax.random.normal(k2, (F, DIM), dtype=jnp.float32)
        bb = jnp.zeros((DIM,), dtype=jnp.float32)
        return {'x': x, 'gamma': gamma, 'beta': beta, 'W': W, 'b': bb}
    _L0_tok_all = _L0_tok_setup()
    _L0_tok_in = {k: v for k, v in _L0_tok_all.items() if k in ('gamma', 'beta', 'W', 'b')}
    del _L0_tok_all

    def _L0_attn_setup():
        import jax, jax.numpy as jnp
        import numpy as np
        NUM_HEADS = 12
        NUM_LANDMARKS = 64
        DIM = 192

        def _iterative_inv(mat, n_iter=6):
            L = mat.shape[-1]
            I = jnp.eye(L, dtype=mat.dtype)
            K = mat
            denom = jnp.max(jnp.sum(K, axis=-2), axis=-1)[:, :, None, None]
            V = 1.0 / denom * jnp.swapaxes(K, -1, -2)
            for _ in range(n_iter):
                KV = jnp.matmul(K, V)
                V = jnp.matmul(0.25 * V, 13.0 * I - jnp.matmul(KV, 15.0 * I - jnp.matmul(KV, 7.0 * I - KV)))
            return V
        key = jax.random.key(seed)
        k1, k2, k3, k4 = jax.random.split(key, 4)
        B, N, C = (4, 1024, DIM)
        x = jax.random.normal(k1, (B, N, C), dtype=jnp.float32)
        w_qkv = jax.random.normal(k2, (3 * C, C), dtype=jnp.float32) * C ** (-0.5)
        w_proj = jax.random.normal(k3, (C, C), dtype=jnp.float32) * C ** (-0.5)
        b_proj = jax.random.normal(k4, (C,), dtype=jnp.float32) * 0.01
        return {'x': x, 'w_qkv': w_qkv, 'w_proj': w_proj, 'b_proj': b_proj}
    _L0_attn_all = _L0_attn_setup()
    _L0_attn_in = {k: v for k, v in _L0_attn_all.items() if k in ('w_qkv', 'w_proj', 'b_proj')}
    del _L0_attn_all

    def _L0_ffn_setup():
        import jax, jax.numpy as jnp
        import numpy as np
        N_EMBD = 192
        EXPERT_SIZES = [(8, 128), (8, 256)]
        TOP_K = 8
        NORM_TOPK_PROB = True
        EXPERT_WIDTHS = []
        for cnt, w in EXPERT_SIZES:
            EXPERT_WIDTHS += [w] * cnt
        EXPERT_OFFSETS = np.concatenate([[0], np.cumsum(EXPERT_WIDTHS)]).astype(np.int64)
        NUM_EXPERTS = len(EXPERT_WIDTHS)
        TOTAL_WIDTH = int(EXPERT_OFFSETS[-1])
        key = jax.random.key(seed)
        k1, k2, k3, k4 = jax.random.split(key, 4)
        x = jax.random.normal(k1, (1, 512, N_EMBD), dtype=jnp.float32)
        router_w = jax.random.normal(k2, (NUM_EXPERTS, N_EMBD), dtype=jnp.float32) * 0.02
        w1 = jnp.clip(jax.random.normal(k3, (N_EMBD, TOTAL_WIDTH), dtype=jnp.float32) * 0.02, -0.06, 0.06)
        w2 = jnp.clip(jax.random.normal(k4, (TOTAL_WIDTH, N_EMBD), dtype=jnp.float32) * 0.02, -0.06, 0.06)
        return {'x': x, 'router_w': router_w, 'w1': w1, 'w2': w2}
    _L0_ffn_all = _L0_ffn_setup()
    _L0_ffn_in = {k: v for k, v in _L0_ffn_all.items() if k in ('router_w', 'w1', 'w2')}
    del _L0_ffn_all
    return {'x': x, 'L0_tok_gamma': _L0_tok_in['gamma'], 'L0_tok_beta': _L0_tok_in['beta'], 'L0_tok_W': _L0_tok_in['W'], 'L0_tok_b': _L0_tok_in['b'], 'L0_attn_w_qkv': _L0_attn_in['w_qkv'], 'L0_attn_w_proj': _L0_attn_in['w_proj'], 'L0_attn_b_proj': _L0_attn_in['b_proj'], 'L0_ffn_router_w': _L0_ffn_in['router_w'], 'L0_ffn_w1': _L0_ffn_in['w1'], 'L0_ffn_w2': _L0_ffn_in['w2']}

def reference(x, L0_tok_gamma, L0_tok_beta, L0_tok_W, L0_tok_b, L0_attn_w_qkv, L0_attn_w_proj, L0_attn_b_proj, L0_ffn_router_w, L0_ffn_w1, L0_ffn_w2):
    import jax
    import jax.numpy as jnp

    def _L0_tok_ref(x, gamma, beta, W, b):
        import jax, jax.numpy as jnp
        import numpy as np
        PATCH = 16
        DIM = 192
        EPS = 0.001

        def _shifts(x):
            zw = jnp.zeros_like(x[:, :, :1, :])
            right = jnp.concatenate([zw, x[:, :, :-1, :]], axis=2)
            left = jnp.concatenate([x[:, :, 1:, :], zw], axis=2)
            zh = jnp.zeros_like(x[:, :1, :, :])
            down = jnp.concatenate([zh, x[:, :-1, :, :]], axis=1)
            up = jnp.concatenate([x[:, 1:, :, :], zh], axis=1)
            return [right, left, down, up]

        def _patchify(x, p):
            b, H, W, C = x.shape
            hh, ww = (H // p, W // p)
            x = x.reshape(b, hh, p, ww, p, C)
            x = x.transpose(0, 1, 3, 2, 4, 5)
            return x.reshape(b, hh * ww, p * p * C)
        x5 = jnp.concatenate([x] + _shifts(x), axis=-1)
        tokens = _patchify(x5, PATCH)
        mu = jnp.mean(tokens, axis=-1, keepdims=True)
        var = jnp.mean(jnp.square(tokens - mu), axis=-1, keepdims=True)
        ln = (tokens - mu) * jax.lax.rsqrt(var + EPS) * gamma + beta
        return jnp.einsum('bnf,fd->bnd', ln, W) + b

    def _L0_attn_ref(x, w_qkv, w_proj, b_proj):
        import jax, jax.numpy as jnp
        import numpy as np
        NUM_HEADS = 12
        NUM_LANDMARKS = 64
        DIM = 192

        def _iterative_inv(mat, n_iter=6):
            L = mat.shape[-1]
            I = jnp.eye(L, dtype=mat.dtype)
            K = mat
            denom = jnp.max(jnp.sum(K, axis=-2), axis=-1)[:, :, None, None]
            V = 1.0 / denom * jnp.swapaxes(K, -1, -2)
            for _ in range(n_iter):
                KV = jnp.matmul(K, V)
                V = jnp.matmul(0.25 * V, 13.0 * I - jnp.matmul(KV, 15.0 * I - jnp.matmul(KV, 7.0 * I - KV)))
            return V
        B, N, C = x.shape
        H, Lm = (NUM_HEADS, NUM_LANDMARKS)
        hd = C // H
        scale = hd ** 0.5
        qkv = (x @ w_qkv.T).reshape(B, N, 3, H, hd).transpose(2, 0, 3, 1, 4)
        q, k, v = (qkv[0], qkv[1], qkv[2])
        q = q / scale
        segs = N // Lm
        keys_landmarks = k.reshape(B, H, Lm, segs, hd).mean(axis=-2)
        queries_landmarks = q.reshape(B, H, Lm, segs, hd).mean(axis=-2)
        kernel_1 = jax.nn.softmax(jnp.einsum('bhnd,bhld->bhnl', q, keys_landmarks), axis=-1)
        kernel_2 = jax.nn.softmax(jnp.einsum('bhmd,bhld->bhml', queries_landmarks, keys_landmarks), axis=-1)
        kernel_3 = jax.nn.softmax(jnp.einsum('bhld,bhnd->bhln', queries_landmarks, k), axis=-1)
        out = jnp.matmul(jnp.matmul(kernel_1, _iterative_inv(kernel_2)), jnp.matmul(kernel_3, v))
        out = out.transpose(0, 2, 1, 3).reshape(B, N, C)
        return out @ w_proj.T + b_proj

    def _L0_ffn_ref(x, router_w, w1, w2):
        import jax, jax.numpy as jnp
        import numpy as np
        N_EMBD = 192
        EXPERT_SIZES = [(8, 128), (8, 256)]
        TOP_K = 8
        NORM_TOPK_PROB = True
        EXPERT_WIDTHS = []
        for cnt, w in EXPERT_SIZES:
            EXPERT_WIDTHS += [w] * cnt
        EXPERT_OFFSETS = np.concatenate([[0], np.cumsum(EXPERT_WIDTHS)]).astype(np.int64)
        NUM_EXPERTS = len(EXPERT_WIDTHS)
        TOTAL_WIDTH = int(EXPERT_OFFSETS[-1])
        B, S, D = x.shape
        xt = x.reshape(-1, D)
        T = xt.shape[0]
        logits = jnp.einsum('td,ed->te', xt, router_w)
        probs = jax.nn.softmax(logits, axis=-1)
        topk_w, topk_idx = jax.lax.top_k(probs, TOP_K)
        if NORM_TOPK_PROB:
            topk_w = topk_w / jnp.sum(topk_w, axis=-1, keepdims=True)
        comb = jnp.zeros((T, NUM_EXPERTS), dtype=xt.dtype)
        comb = comb.at[jnp.arange(T)[:, None], topk_idx].add(topk_w)
        out = jnp.zeros_like(xt)
        for e in range(NUM_EXPERTS):
            off = int(EXPERT_OFFSETS[e])
            wd = EXPERT_WIDTHS[e]
            h = jax.nn.gelu(xt @ w1[:, off:off + wd])
            out = out + comb[:, e:e + 1] * (h @ w2[off:off + wd, :])
        return out.reshape(B, S, D)
    h = _L0_tok_ref(x, L0_tok_gamma, L0_tok_beta, L0_tok_W, L0_tok_b)
    h = h + _L0_attn_ref(_layernorm(h, axis=-1), L0_attn_w_qkv, L0_attn_w_proj, L0_attn_b_proj)
    h = h + _L0_ffn_ref(_layernorm(h, axis=-1), L0_ffn_router_w, L0_ffn_w1, L0_ffn_w2)
    return h

_drawn_inputs = setup_inputs


def setup_inputs(seed=0):
    import zlib

    import numpy as np

    out = dict(_drawn_inputs(seed))
    spreads = {'L0_tok_gamma': (1.0, 0.2), 'L0_tok_beta': (0.0, 0.1), 'L0_tok_b': (0.0, 0.8)}
    factors = {'L0_attn_w_qkv': 8.0,
     'L0_attn_w_proj': 8.0,
     'L0_attn_b_proj': 64.0,
     'L0_ffn_router_w': 21.633,
     'L0_ffn_w1': 23.23,
     'L0_ffn_w2': 8.0}
    for name, (base, spread) in spreads.items():
        noise = np.random.default_rng([zlib.crc32(name.encode()), seed]).standard_normal(out[name].shape)
        drawn = base * np.exp(spread * noise) if base else spread * noise
        out[name] = jnp.asarray(drawn.astype(out[name].dtype))
    for name, factor in factors.items():
        out[name] = (out[name] * factor).astype(out[name].dtype)
    return out
```

```python
from contextlib import ExitStack

import concourse.bass as bass
from concourse import mybir

P = 128
IMGS, TOK, DIM = 32, 64, 192
HEADS, HD = 12, 16
PAIRS = HEADS // 2
NT = IMGS * TOK // P
FEAT = 3840
CH = 8
DA, DB = 128, DIM - 128
STEPS = 6
EXPERTS, TOPK = 16, 8
WIDTH = [1] * 8 + [2] * 8
HID = sum(WIDTH)
RSQ = 16
GT = 4
ROW = 80

F32 = mybir.dt.float32
I32 = mybir.dt.int32
F32R = mybir.dt.float32r
ALU = mybir.AluOpType
ACT = mybir.ActivationFunctionType
AX = mybir.AxisListType.X

C_ID, C_EYE, C_HM, C_PC, C_MULT = 0, 128, 192, 204, 212
C_ALL = C_MULT + CH * P


def later(t):
    return not isinstance(t, int) or t > 0


def vit_block_kernel(nc, x, ws, wh, gb, tok_b, wqk, wv, wp, bp, rw, w1, w2, const, out):
    with ExitStack() as ctx:
        def sb(name, shape, dtype=F32):
            return ctx.enter_context(nc.sbuf_tensor(name, shape, dtype))

        def sem(name):
            return ctx.enter_context(nc.semaphore(name))

        cst = sb("cst", [P, C_ALL])
        ident = cst[:, C_ID:C_ID + P]
        eye = cst[:, C_EYE:C_EYE + 64]
        head_mask = cst[:, C_HM:C_HM + HEADS]
        pc = cst[:, C_PC:C_PC + 8]
        mult = cst[:, C_MULT:C_MULT + CH * P]
        wsh = sb("wsh", [P, 2, 5, 3, DIM])
        whalo = sb("whalo", [P, 2, DIM])
        gbs = sb("gbs", [P, 2, 32])
        weff = sb("weff", [P, CH, DIM])
        crow = sb("crow", [1, DIM])
        ones = sb("ones", [1, P])
        tokb = sb("tokb", [P, DIM])
        cvec = sb("cvec", [P, DIM])
        wqk_a, wqk_b = sb("wqk_a", [DA, 2 * DIM]), sb("wqk_b", [DB, 2 * DIM])
        wv_a, wv_b = sb("wv_a", [DA, DIM]), sb("wv_b", [DB, DIM])
        wp_sb = sb("wp_sb", [P, 4, DIM])
        bp_sb = sb("bp_sb", [P, DIM])
        rw_a, rw_b = sb("rw_a", [DA, EXPERTS]), sb("rw_b", [DB, EXPERTS])
        w1_a, w1_b = sb("w1_a", [DA, HID * P]), sb("w1_b", [P, HID * P])
        w2_sb = sb("w2_sb", [P, HID, DIM])

        work = sb("work", [P, 2 * CH * P])
        xin = work[:, 0:CH * P]
        xc = work[:, CH * P:].rearrange("p (c n) -> p c n", n=P)
        sq = sb("sq", [P, CH * P])
        xct = sb("xct", [P, CH, P])
        scrap = sb("scrap", [P, 4])
        st = sb("st", [P, 24])
        h_t = sb("h_t", [P, DIM])
        xl = sb("xl", [P, DIM])
        xlt = sb("xlt", [P, 2, P])
        bn = sb("bn", [P, 8])
        qt = sb("qt", [P, 2, P])
        kb_a = sb("kb_a", [P, 2, 8, 64])
        kb_b = sb("kb_b", [DB, 2, 4, 64])
        se = sb("se", [P, HEADS, 64])
        sst = sb("sst", [P, 3, HEADS])
        kv = sb("kv", [P, 2, PAIRS, 2, ROW])
        csum = sb("csum", [P, PAIRS, 2])
        dmx = sb("dmx", [HEADS, 2, 2])
        dbc = sb("dbc", [HEADS, 2, 64])
        nid = sb("nid", [P, PAIRS, 2])
        m0 = sb("m0", [P, 2, PAIRS, 64])
        r0 = sb("r0", [P, 2, PAIRS, 2, 64])
        rr = sb("rr", [P, 2, PAIRS, 2, 64])
        uu = sb("uu", [P, 2, PAIRS, 2, 64])
        qq = sb("qq", [P, 2, PAIRS, 64])
        y_t = sb("y_t", [P, 2, PAIRS, 32])
        ot = sb("ot", [P, 2, 2, P])
        h2 = sb("h2", [P, DIM])
        x2 = sb("x2", [P, 2 * P])
        x2t = sb("x2t", [P, 2, P])
        bn2 = sb("bn2", [P, 8])
        rt = sb("rt", [P, 4, EXPERTS])
        rst = sb("rst", [P, 12])
        acc = sb("acc", [P, NT, DIM])
        comb = sb("comb", [P, NT, EXPERTS])
        xhi, xlo = sb("xhi", [P, 2, NT * P], F32R), sb("xlo", [P, 2, NT * P], F32R)
        hid = work[:].rearrange("p (c n) -> p c n", c=4)
        wah, wal, wb = (sb(n, [P, 3, P], F32R) for n in ("wah", "wal", "wb"))

        ps = ctx.enter_context(nc.psum_tensor("ps", [P, 8, 512], F32))
        NB = [ps[:, i, 0:PAIRS * 64].rearrange("p (h n) -> p h n", h=PAIRS) for i in (0, 1)]
        SA, SB_, TA, TB, M6, M7 = (ps[:, i, :] for i in (2, 3, 4, 5, 6, 7))

        def sems(names):
            return [sem(n) for n in names.split()]

        const_loaded, wsh_loaded, x_loaded = sems("const_loaded wsh_loaded x_loaded")
        attw_loaded, ffw_loaded, x_free, ones_set = sems("attw_loaded ffw_loaded x_free ones_set")
        scrap_set, zeros_set, folded, beta_done = sems("scrap_set zeros_set folded beta_done")
        crow_ready, cbc_done, cvec_ready, xmean = sems("crow_ready cbc_done cvec_ready xmean")
        xmean2, xc_ready, sq_ready, xvar, xrstd = sems("xmean2 xc_ready sq_ready xvar xrstd")
        xtr_done, xct_ready, tok_done, h_ready = sems("xtr_done xct_ready tok_done h_ready")
        res_saved, bn_a, bn_b, lrstd, xl_ready = sems("res_saved bn_a bn_b lrstd xl_ready")
        xltr_done, xlt_ready, qk_done, q_copied = sems("xltr_done xlt_ready qk_done q_copied")
        kb_ready, v_done, v_copied, scores_done, smax = sems("kb_ready v_done v_copied scores_done smax")
        sdiff, probs_exp, psumd, prec, kn_ready = sems("sdiff probs_exp psumd prec kn_ready")
        kt_done, colsum_a, colsum_b, kt_copied = sems("kt_done colsum_a colsum_b kt_copied")
        cst_done, dmax, drec, dbc_ready, dbt_done = sems("cst_done dmax drec dbc_ready dbt_done")
        nid_ready, m0_done, m0_scaled, r0_ready = sems("nid_ready m0_done m0_scaled r0_ready")
        r0_last_ready, y_copied, square_done = sems("r0_last_ready y_copied square_done")
        q_ready, u_ready, prod_done, r_ready, o_done = sems("q_ready u_ready prod_done r_ready o_done")
        o_copied, proj_done, h2_ready, h2_saved = sems("o_copied proj_done h2_ready h2_saved")
        tbn_a, tbn_b, trstd, x2_ready, x2tr_done = sems("tbn_a tbn_b trstd x2_ready x2tr_done")
        x2t_ready, xhi_ready, x2_saved, logits_done = sems("x2t_ready xhi_ready x2_saved logits_done")
        lmax, lexp, ltop, lrep, lsel, lsum, linv = sems("lmax lexp ltop lrep lsel lsum linv")
        comb_ready, whi_ready, wlo_ready, up_done = sems("comb_ready whi_ready wlo_ready up_done")
        gelu_done, down_done, expert_added = sems("gelu_done down_done expert_added")
        out_stored, = sems("out_stored")

        block = ctx.enter_context(nc.Block())

        def wait_first(semaphore, value):
            nc.vector.wait_ge(semaphore, value)
            nc.vector.tensor_copy(scrap[:, 0:1], scrap[:, 1:2])

        @block.sync
        def _(sp):
            sp.dma_start(cst[:], const).then_inc(const_loaded, 16)
            sp.dma_start(gbs[:], gb).then_inc(wsh_loaded, 16)
            sp.dma_start(wsh[:], ws).then_inc(wsh_loaded, 16)
            sp.dma_start(whalo[:], wh).then_inc(wsh_loaded, 16)
            sp.dma_start(tokb[:], tok_b.partition_broadcast(P)).then_inc(wsh_loaded, 16)
            sp.dma_start(xin, x[0]).then_inc(x_loaded, 16)
            sp.dma_start(wqk_a[:], wqk[0:DA, :]).then_inc(attw_loaded, 16)
            sp.dma_start(wqk_b[:], wqk[DA:DIM, :]).then_inc(attw_loaded, 16)
            sp.dma_start(wv_a[:], wv[0:DA, :]).then_inc(attw_loaded, 16)
            sp.dma_start(wv_b[:], wv[DA:DIM, :]).then_inc(attw_loaded, 16)
            sp.dma_start(wp_sb[:], wp).then_inc(attw_loaded, 16)
            sp.dma_start(bp_sb[:], bp.partition_broadcast(P)).then_inc(attw_loaded, 16)
            sp.dma_start(rw_a[:], rw[0:DA, :]).then_inc(attw_loaded, 16)
            sp.dma_start(rw_b[:], rw[DA:DIM, :]).then_inc(attw_loaded, 16)
            sp.wait_ge(x_free, 1)
            sp.dma_start(xin, x[1]).then_inc(x_loaded, 16)
            sp.dma_start(w1_a[:], w1[0:DA, :]).then_inc(ffw_loaded, 16)
            sp.dma_start(w1_b[0:DB, :], w1[DA:DIM, :]).then_inc(ffw_loaded, 16)
            sp.dma_start(w1_b[DB:P, :], w1[DA:DIM, :]).then_inc(ffw_loaded, 16)
            sp.dma_start(w2_sb[:], w2.rearrange("(c p) n -> p c n", p=P)).then_inc(ffw_loaded, 16)
            with sp.Fori(2, NT) as t:
                sp.wait_ge(x_free, t)
                sp.dma_start(xin, x[bass.ds(t, 1)].rearrange("a p f -> (a p) f")).then_inc(x_loaded, 16)
            with sp.Fori(0, NT // GT) as g:
                sp.wait_ge(expert_added, (g + 1) * EXPERTS + 2)
                sp.dma_start(out[bass.ds(g * GT, GT)].rearrange("t p n -> p t n"),
                             acc[:, bass.ds(g * GT, GT), :]).then_inc(out_stored, 16)
            sp.wait_ge(out_stored, 16 * (NT // GT))

        @block.gpsimd
        def _(pool):
            pool.memset(ones[:], 1.0).then_inc(ones_set, 1)
            for buf in (r0, rr, uu, kv, y_t):
                pool.memset(buf[:], 0.0).then_inc(zeros_set, 1)

            def front_last(t):
                pool.wait_ge(m0_scaled, 2 * t + 2)
                pool.tensor_tensor(r0[64:P, 1, :, 1, :], m0[64:P, 1, :, :],
                                   eye[64:P, :].unsqueeze(1).to_broadcast([64, PAIRS, 64]),
                                   ALU.add).then_inc(r0_last_ready, 1)

            def rsqrt(out_, var, scale_eps, w, steps, t):
                n = [t * RSQ]

                def step(op, wait=True):
                    op.then_inc(steps, 1)
                    n[0] = n[0] + 1
                    if wait:
                        pool.wait_ge(steps, n[0])
                v, hv, a, y = (w[:, k:k + 1] for k in range(4))
                c = scale_eps
                step(pool.tensor_tensor(v, var, pc[:, c:c + 1], ALU.mult))
                step(pool.tensor_tensor(v, v, pc[:, c + 1:c + 2], ALU.add))
                step(pool.tensor_tensor(hv, v, pc[:, 4:5], ALU.mult), wait=False)
                step(pool.tensor_scalar(y.bitcast(I32), v.bitcast(I32), -0.5, float(0x5f3759df), ALU.mult, ALU.add))
                for k in range(3):
                    step(pool.tensor_tensor(a, y, y, ALU.mult))
                    step(pool.tensor_tensor(a, a, hv, ALU.mult))
                    step(pool.tensor_tensor(a, a, pc[:, 5:6], ALU.add))
                    step(pool.tensor_tensor(out_ if k == 2 else y, a, y, ALU.mult))

            def front(s, t):
                if s == 0:
                    pool.wait_ge(xvar, t + 1)
                    rsqrt(st[:, 4:5], st[:, 2:3], 0, st[:, 8:13], xrstd, t)
                if s == 1:
                    pool.wait_ge(bn_b, t + 1)
                    rsqrt(st[:, 5:6], bn[:, 7:8], 2, st[:, 16:21], lrstd, t)

            def tail(s, t):
                if s == 1:
                    pool.wait_ge(tbn_b, t + 1)
                    rsqrt(rst[:, 1:2], bn2[:, 7:8], 2, rst[:, 4:9], trstd, t)
                if s == 3:
                    pool.wait_ge(h2_ready, t + 1)
                    pool.tensor_copy(acc[:, bass.ds(t, 1), :], h2[:].unsqueeze(1)).then_inc(h2_saved, 1)
                if s == 4:
                    pool.wait_ge(xhi_ready, t + 1)
                    pool.tensor_tensor(xlo[:, :, bass.ds(t * P, P)], x2t[:], xhi[:, :, bass.ds(t * P, P)].bitcast(F32),
                                       ALU.subtract).then_inc(x2_saved, 1)

            def iteration(t, front_on=True, tail_on=True):
                pool.wait_ge(r0_last_ready, t + 1)
                for s in range(5):
                    if tail_on:
                        tail(s, t - 1)
                    if front_on:
                        front(s, t + 1)
                if tail_on:
                    pool.wait_ge(x2_saved, t)
                if front_on:
                    front_last(t + 1)

            pool.wait_ge(const_loaded, 16)
            pool.wait_ge(zeros_set, 5)
            for s in range(5):
                front(s, 0)
            front_last(0)
            iteration(0, tail_on=False)
            with pool.Fori(1, NT - 1) as t:
                iteration(t)
            iteration(NT - 1, front_on=False)
            for s in range(5):
                tail(s, NT - 1)

        @block.tensor
        def _(pe):
            def front(s, t):
                if s == 0:
                    pe.wait_ge(xc_ready, t + 1)
                    if later(t):
                        pe.wait_ge(kt_copied, 4 * t)
                    for c in range(CH):
                        last = pe.transpose((TA, TB)[c // 4][:, (c % 4) * P:(c % 4 + 1) * P], xc[:, c, :], ident)
                        if c % 4 == 3:
                            last.then_inc(xtr_done, 1)
                if s == 1:
                    pe.wait_ge(xct_ready, 2 * t + 2)
                    for c in range(CH):
                        last = pe.matmul(M7[:, 0:DIM], xct[:, c, :], weff[:, c, :], start=(c == 0), stop=(c == CH - 1))
                    last.then_inc(tok_done, 1)
                if s == 4:
                    pe.wait_ge(xl_ready, t + 1)
                    pe.transpose(M6[:, 0:P], xl[:, 0:DA], ident)
                    pe.transpose(M6[0:DB, P:2 * P], xl[:, DA:DIM], ident).then_inc(xltr_done, 1)
                if s == 5:
                    pe.wait_ge(xlt_ready, 2 * t + 2)
                    for n, (c0, m) in enumerate(((0, DA), (DA, DB), (DIM, DA), (DIM + DA, DB))):
                        pe.matmul(M7[0:m, n * P:(n + 1) * P], wqk_a[:, c0:c0 + m], xlt[:, 0, :], start=True, stop=False)
                        last = pe.matmul(M7[0:m, n * P:(n + 1) * P], wqk_b[:, c0:c0 + m], xlt[0:DB, 1, :],
                                         start=False, stop=True)
                    last.then_inc(qk_done, 1)
                if s == 6:
                    pe.matmul(M6[:, 0:DIM], xlt[:, 0, :], wv_a[:], start=True, stop=False)
                    pe.matmul(M6[:, 0:DIM], xlt[0:DB, 1, :], wv_b[:], start=False, stop=True).then_inc(v_done, 1)
                if s == 7:
                    pe.wait_ge(q_copied, 2 * t + 2)
                    pe.wait_ge(kb_ready, 4 * t + 4)
                    for i in range(2):
                        r = slice(64 * i, 64 * i + 64)
                        pe.matmul(SA[r, :], qt[:, 0, r], kb_a[:, i].rearrange("p h n -> p (h n)"), start=True, stop=True)
                        last = pe.matmul(SB_[r, 0:256], qt[0:DB, 1, r], kb_b[:, i].rearrange("p h n -> p (h n)"),
                                         start=True, stop=True)
                    last.then_inc(scores_done, 1)
                if s == 9:
                    pe.wait_ge(kn_ready, t + 1)
                    for p in range(PAIRS):
                        last = pe.transpose((TA, TB)[p // 4][:, (p % 4) * P:(p % 4 + 1) * P],
                                            se[:, 2 * p:2 * p + 2, :].rearrange("p h n -> p (h n)"), ident)
                        if p in (3, PAIRS - 1):
                            last.then_inc(kt_done, 1)
                if s == 10:
                    pe.wait_ge(colsum_a, t + 1)
                    pe.wait_ge(colsum_b, t + 1)
                    pe.wait_ge(v_copied, 4 * t + 4)
                    pe.transpose(M6[0:HEADS, 0:P], csum[:].rearrange("p h i -> p (h i)"), ident).then_inc(cst_done, 1)
                if s == 11:
                    pe.wait_ge(dbc_ready, t + 1)
                    pe.matmul(M7[:, 0:HEADS], dbc[:].rearrange("p h n -> p (h n)"), ident[0:HEADS, 0:HEADS],
                              start=True, stop=True).then_inc(dbt_done, 1)

            def front_last(t):
                pe.wait_ge(kt_copied, 4 * t + 4)
                pe.wait_ge(sdiff, 2 * t + 2)
                for i in range(2):
                    for p in range(PAIRS):
                        for half in range(2):
                            r = slice(64 * half, 64 * half + 64)
                            last = pe.matmul((SA, SB_)[i][r, p * ROW:(p + 1) * ROW], kv[:, i, p, half, 0:64],
                                             kv[:, i, p, half, :], start=True, stop=True)
                    last.then_inc(m0_done, 1)

            def newton(k, phase, t):
                for i in range(2):
                    n = 12 * t + 2 * k + i
                    src = r0 if k == 0 else rr
                    for half in range(2):
                        r = slice(64 * half, 64 * half + 64)
                        if phase == 0:
                            if k > 0:
                                pe.wait_ge(r_ready, 2 * n - 3 + half)
                            elif i == half == 1:
                                pe.wait_ge(r0_last_ready, t + 1)
                            else:
                                pe.wait_ge(r0_ready, 3 * t + 2 * i + half + 1)
                        else:
                            pe.wait_ge(u_ready, 2 * n + half + 1)
                        for p in range(PAIRS):
                            lhs = src[:, i, p, half, :] if phase == 0 else qq[:, i, p, :]
                            rhs = src[:, i, p, half, :] if phase == 0 else uu[:, i, p, half, :]
                            last = pe.matmul(NB[i][r, p, :], lhs, rhs, start=True, stop=True)
                    last.then_inc((square_done, prod_done)[phase], 1)

            def tail(s, t):
                if s == 0:
                    pe.wait_ge(r_ready, 24 * t + 24)
                    pe.wait_ge(y_copied, 2 * t + 2)
                    for i in range(2):
                        for p in range(PAIRS):
                            g, j = divmod(p, 4)
                            o = M7[32 * j:32 * j + 32, g * 256:(g + 1) * 256].rearrange("p (h i n) -> p h i n", h=2, i=2)
                            last = pe.matmul(o[:, :, i, :], y_t[:, i, p, :], rr[:, i, p].rearrange("p h n -> p (h n)"),
                                             start=True, stop=True, tile_position=(0, 32 * j))
                    last.then_inc(o_done, 1)
                if s == 1:
                    pe.wait_ge(o_copied, 2 * t + 2)
                    for g in range(2):
                        rows = P if g == 0 else 64
                        for half in range(2):
                            last = pe.matmul(M6[:, 0:DIM], ot[0:rows, g, half, :], wp_sb[0:rows, 2 * g + half, :],
                                             start=(g + half == 0), stop=(g + half == 2))
                    last.then_inc(proj_done, 1)
                if s == 4:
                    pe.wait_ge(x2_ready, 2 * t + 2)
                    pe.transpose(M7[:, 0:P], x2[:, 0:DA], ident)
                    pe.transpose(M7[:, P:2 * P], x2[:, DA:], ident).then_inc(x2tr_done, 1)
                if s == 5:
                    pe.wait_ge(x2t_ready, t + 1)
                    pe.matmul(SA[:, 0:EXPERTS], x2t[:, 0, :], rw_a[:], start=True, stop=False)
                    pe.matmul(SA[:, 0:EXPERTS], x2t[0:DB, 1, :], rw_b[:], start=False, stop=True).then_inc(logits_done, 1)

            def bank_waits(s, t, front_on, tail_on):
                if s == 4 and front_on and tail_on:
                    pe.wait_ge(h2_ready, t)
                if s == 4 and tail_on and front_on:
                    pe.wait_ge(h_ready, t + 2)
                if s == 5 and tail_on and front_on:
                    pe.wait_ge(xhi_ready, t)
                if s == 7 and tail_on and front_on:
                    pe.wait_ge(lexp, t)

            def iteration(t, front_on=True, tail_on=True):
                for s in range(2 * STEPS):
                    newton(s // 2, s % 2, t)
                    if s == 5:
                        pe.wait_ge(y_copied, 2 * t + 2)
                    if s == 1 and front_on and tail_on:
                        pe.wait_ge(o_copied, 2 * t)
                    if tail_on:
                        bank_waits(s, t, front_on, tail_on)
                        tail(s, t - 1)
                    if front_on:
                        front(s, t + 1)
                if front_on:
                    front_last(t + 1)

            pe.wait_ge(const_loaded, 16)
            pe.wait_ge(wsh_loaded, 64)
            n = 0
            for hh in range(2):
                for f in range(15):
                    pe.matmul(M6[0:1, 0:DIM], gbs[:, 1, hh * 15 + f:hh * 15 + f + 1], wsh[:, hh, f // 3, f % 3, :],
                              start=(n == 0), stop=False)
                    n += 1
            pe.matmul(M6[0:1, 0:DIM], gbs[:, 1, 30:31], whalo[:, 0, :], start=False, stop=False)
            pe.matmul(M6[0:1, 0:DIM], gbs[:, 1, 31:32], whalo[:, 1, :], start=False, stop=True).then_inc(beta_done, 1)
            pe.wait_ge(crow_ready, 1)
            pe.wait_ge(ones_set, 1)
            pe.matmul(M7[:, 0:DIM], ones[:], crow[:], start=True, stop=True).then_inc(cbc_done, 1)
            pe.wait_ge(cvec_ready, 1)
            pe.wait_ge(folded, 32)
            pe.wait_ge(attw_loaded, 16 * 8)
            for s in range(2 * STEPS):
                front(s, 0)
            front_last(0)
            iteration(0, tail_on=False)
            with pe.Fori(1, NT - 1) as t:
                iteration(t)
            iteration(NT - 1, front_on=False)
            for s in range(2 * STEPS):
                tail(s, NT - 1)

            pe.wait_ge(ffw_loaded, 64)
            pe.wait_ge(x2_saved, NT)
            pe.wait_ge(comb_ready, NT)
            first = [sum(WIDTH[:e]) for e in range(EXPERTS)]
            with pe.Fori(0, NT // GT) as g:
                def up(c):
                    pe.wait_ge(whi_ready, (g * HID + c + 1) * 2)
                    pe.wait_ge(wlo_ready, (g * HID + c + 1) * 2)
                    if c >= 2:
                        pe.wait_ge(gelu_done, g * HID + (c - 1))
                    tok = bass.ds(g * GT * P, GT * P)
                    k = c % 3
                    parts = ((wah, xhi, 0), (wah, xlo, 0), (wal, xhi, 0), (wb, xhi, 1), (wb, xlo, 1))
                    for n, (w, xs, half) in enumerate(parts):
                        last = pe.matmul(ps[:, c % 2, :], w[:, k, :], xs[:, half, tok], start=(n == 0), stop=(n == 4))
                    last.then_inc(up_done, 1)

                def down(e, c):
                    if c == first[e]:
                        pe.wait_ge(expert_added, g * EXPERTS + e + 1)
                    pe.wait_ge(gelu_done, g * HID + c + 1)
                    for j in range(GT):
                        last = pe.matmul(ps[:, 2 + 2 * (e % 2) + j // 2, (j % 2) * DIM:(j % 2 + 1) * DIM],
                                         hid[:, c % 4, j * P:(j + 1) * P], w2_sb[:, c, :],
                                         start=(c == first[e] and j % 2 == 0), stop=(c == first[e] + WIDTH[e] - 1),
                                         skip_group_check=True)
                    if c == first[e] + WIDTH[e] - 1:
                        last.then_inc(down_done, 1)
                chunks = [(e, first[e] + w) for e in range(EXPERTS) for w in range(WIDTH[e])]
                up(0)
                for e, c in chunks:
                    if c + 1 < HID:
                        up(c + 1)
                    down(e, c)

        @block.scalar
        def _(act):
            def squares(t):
                act.wait_ge(xc_ready, t + 1)
                act.activation(sq[:], xc.rearrange("p c n -> p (c n)"), ACT.Square).then_inc(sq_ready, 1)

            def front(s, t):
                if s == 0:
                    for n, b in enumerate((TA, TB)):
                        act.wait_ge(xtr_done, 2 * t + n + 1)
                        act.activation(xct[:, 4 * n:4 * n + 4, :].rearrange("p c n -> p (c n)"), b,
                                       ACT.Copy).then_inc(xct_ready, 1)
                if s == 4:
                    act.wait_ge(xltr_done, t + 1)
                    act.activation(xlt[:, 0, :], M6[:, 0:P], ACT.Copy).then_inc(xlt_ready, 1)
                    act.activation(xlt[0:DB, 1, :], M6[0:DB, P:2 * P], ACT.Copy).then_inc(xlt_ready, 1)
                if s == 5:
                    act.wait_ge(qk_done, t + 1)
                    act.activation(qt[:, 0, :], M7[:, 0:P], ACT.Copy).then_inc(q_copied, 1)
                    act.activation(qt[0:DB, 1, :], M7[0:DB, P:2 * P], ACT.Copy).then_inc(q_copied, 1)
                if s == 6:
                    act.wait_ge(v_done, t + 1)
                    for i in range(2):
                        for half in range(2):
                            act.activation(kv[64 * half:64 * half + 64, i, :, half, 64:ROW],
                                           M6[64 * i:64 * i + 64, half * 96:half * 96 + 96].rearrange(
                                               "p (h d) -> p h d", d=HD), ACT.Copy).then_inc(v_copied, 1)
                if s == 8:
                    act.wait_ge(sdiff, 2 * t + 2)
                    act.activation(se[:], se[:], ACT.Exp, scale=1.0 / (HD ** 0.5)).then_inc(probs_exp, 1)
                if s == 9:
                    for bank, (b, p0, np_, cs) in enumerate(((TA, 0, 4, colsum_a), (TB, 4, 2, colsum_b))):
                        act.wait_ge(cs, t + 1)
                        for half in range(2):
                            a, z = 64 * half, 64 * half + 64
                            act.activation(kv[a:z, :, p0:p0 + np_, half, 0:64].rearrange("p i h n -> p h i n"),
                                           b[a:z, 0:np_ * P].rearrange("p (h i n) -> p h i n", i=2, n=64),
                                           ACT.Copy).then_inc(kt_copied, 1)

            def save_y(t):
                if later(t):
                    act.wait_ge(o_done, t)
                for i in range(2):
                    act.wait_ge(m0_scaled, 2 * t + i + 1)
                    act.activation(y_t[:, i, :, 0:HD],
                                   (SA, SB_)[i][:, 0:PAIRS * ROW].rearrange("p (h c) -> p h c", c=ROW)[:, :, 64:ROW],
                                   ACT.Copy).then_inc(y_copied, 1)

            def newton(k, phase, t):
                for i in range(2):
                    n = 12 * t + 2 * k + i
                    if phase == 0:
                        act.wait_ge(square_done, n + 1)
                        act.activation(qq[:, i], NB[i], ACT.Copy).then_inc(q_ready, 1)
                    elif k < STEPS - 1:
                        act.wait_ge(prod_done, n + 1)
                        for half in range(2):
                            a, z = 64 * half, 64 * half + 64
                            act.activation(rr[a:z, i, :, half, :], NB[i][a:z], ACT.Copy, scale=0.25).then_inc(r_ready, 1)

            def tail(s, t):
                if s == 0:
                    act.wait_ge(o_done, t + 1)
                    act.activation(ot[:, 0].rearrange("p h n -> p (h n)"), M7[:, 0:256], ACT.Copy).then_inc(o_copied, 1)
                    act.activation(ot[0:64, 1].rearrange("p h n -> p (h n)"), M7[0:64, 256:512],
                                   ACT.Copy).then_inc(o_copied, 1)
                if s == 4:
                    act.wait_ge(x2tr_done, t + 1)
                    if later(t):
                        act.wait_ge(x2_saved, t)
                    m7 = M7[:, 0:2 * P].rearrange("p (a n) -> p a n", a=2)
                    act.activation(x2t[:], m7, ACT.Copy).then_inc(x2t_ready, 1)
                    act.activation(xhi[:, :, bass.ds(t * P, P)], m7, ACT.Copy).then_inc(xhi_ready, 1)
                if s == 5:
                    act.wait_ge(lmax, t + 1)
                    act.activation(rt[:, 0, :], SA[:, 0:EXPERTS], ACT.Exp, bias=rst[:, 0:1]).then_inc(lexp, 1)

            def iteration(t, centre_on=True, front_on=True, tail_on=True):
                for s in range(2 * STEPS):
                    newton(s // 2, s % 2, t)
                    if s == 1:
                        save_y(t)
                    if tail_on:
                        tail(s, t - 1)
                    if front_on:
                        front(s, t + 1)
                    if s == 10 and centre_on:
                        squares(t + 2)

            act.wait_ge(zeros_set, 5)
            squares(0)
            for s in range(2 * STEPS):
                front(s, 0)
                if s == 10:
                    squares(1)
            iteration(0, tail_on=False)
            with act.Fori(1, NT - 2) as t:
                iteration(t)
            iteration(NT - 2, centre_on=False)
            iteration(NT - 1, centre_on=False, front_on=False)
            for s in range(2 * STEPS):
                tail(s, NT - 1)
            act.wait_ge(ffw_loaded, 64)
            with act.Fori(0, NT // GT) as g:
                expert_of = [e for e in range(EXPERTS) for _ in range(WIDTH[e])]

                def high_part(c):
                    for w, raw in ((wah, w1_a), (wb, w1_b)):
                        act.activation(w[:, c % 3, :], raw[:, c * P:(c + 1) * P], ACT.Copy).then_inc(whi_ready, 1)
                high_part(0)
                high_part(1)
                for c in range(HID):
                    if c + 2 < HID:
                        if c >= 1:
                            act.wait_ge(up_done, g * HID + c)
                        high_part(c + 2)
                    act.wait_ge(up_done, g * HID + c + 1)
                    if c >= 4:
                        act.wait_ge(down_done, g * EXPERTS + expert_of[c - 4] + 1)
                    act.activation(hid[:, c % 4, :], ps[:, c % 2, :], ACT.Gelu_apprx_tanh).then_inc(gelu_done, 1)
                act.wait_ge(down_done, (g + 1) * EXPERTS)

        @block.vector
        def _(dve):
            def centre(t):
                dve.wait_ge(x_loaded, 16 * t + 16)
                dve.tensor_tensor_reduce(out=sq[:], in0=xin, in1=mult, scale=1.0, scalar=0.0, op0=ALU.mult,
                                         op1=ALU.add, accum_out=st[:, 0:1]).then_inc(xmean, 1)
                dve.wait_ge(xmean, t + 1)
                dve.tensor_scalar(st[:, 1:2], st[:, 0:1], 1.0 / FEAT, None, ALU.mult).then_inc(xmean2, 1)
                dve.wait_ge(xmean2, t + 1)
                if later(t):
                    dve.wait_ge(xtr_done, 2 * t)
                dve.tensor_scalar(xc.rearrange("p c n -> p (c n)"), xin, st[:, 1:2], None,
                                  ALU.subtract).then_inc(xc_ready, 1)
                dve.wait_ge(xc_ready, t + 1)
                dve.sem_inc(x_free, 1)

            def front(s, t):
                if s == 0:
                    dve.wait_ge(sq_ready, t + 1)
                    dve.tensor_tensor_reduce(out=sq[:], in0=sq[:], in1=mult, scale=1.0, scalar=0.0, op0=ALU.mult,
                                             op1=ALU.add, accum_out=st[:, 2:3]).then_inc(xvar, 1)
                if s == 1:
                    dve.wait_ge(tok_done, t + 1)
                    dve.wait_ge(xrstd, RSQ * (t + 1))
                    dve.scalar_tensor_tensor(out=h_t[:], in0=M7[:, 0:DIM], scalar=st[:, 4:5], in1=cvec[:],
                                             op0=ALU.mult, op1=ALU.add).then_inc(h_ready, 1)
                    dve.wait_ge(h_ready, t + 1)
                    dve.bn_stats(bn[:, 0:6], h_t[:]).then_inc(bn_a, 1)
                    dve.wait_ge(bn_a, t + 1)
                    dve.tensor_tensor(acc[:, bass.ds(t, 1), :], h_t[:].unsqueeze(1), bp_sb[:].unsqueeze(1),
                                      ALU.add).then_inc(res_saved, 1)
                    dve.bn_aggr(bn[:, 6:8], bn[:, 0:6]).then_inc(bn_b, 1)
                if s == 3:
                    dve.wait_ge(lrstd, RSQ * (t + 1))
                    dve.tensor_scalar(xl[:], h_t[:], bn[:, 6:7], st[:, 5:6], ALU.subtract, ALU.mult).then_inc(xl_ready, 1)
                if s == 5:
                    dve.wait_ge(q_copied, 2 * t + 2)
                    for i in range(2):
                        for buf, rows, col, nh, h0 in ((kb_a, P, 2 * P, 8, 0), (kb_b, DB, 3 * P, 4, 8)):
                            dve.tensor_tensor(buf[:, i], M7[0:rows, col + 64 * i:col + 64 * i + 64].unsqueeze(1)
                                              .to_broadcast([rows, nh, 64]),
                                              head_mask[0:rows, h0:h0 + nh].unsqueeze(2).to_broadcast([rows, nh, 64]),
                                              ALU.mult).then_inc(kb_ready, 1)
                if s == 7:
                    dve.wait_ge(scores_done, t + 1)
                    sa = SA.rearrange("p (h n) -> p h n", n=64)
                    sb_ = SB_[:, 0:256].rearrange("p (h n) -> p h n", n=64)
                    dve.tensor_reduce(sst[:, 0, 0:8], sa, AX, ALU.max).then_inc(smax, 1)
                    dve.tensor_reduce(sst[:, 0, 8:12], sb_, AX, ALU.max).then_inc(smax, 1)
                    for n, (src, h0, nh) in enumerate(((sa, 0, 8), (sb_, 8, 4))):
                        dve.wait_ge(smax, 2 * t + 1 + n)
                        dve.tensor_tensor(se[:, h0:h0 + nh, :], src, sst[:, 0, h0:h0 + nh].unsqueeze(2)
                                          .to_broadcast([P, nh, 64]), ALU.subtract).then_inc(sdiff, 1)
                if s == 8:
                    dve.wait_ge(probs_exp, t + 1)
                    dve.tensor_reduce(sst[:, 1, :], se[:], AX, ALU.add).then_inc(psumd, 1)
                    dve.wait_ge(psumd, t + 1)
                    dve.reciprocal(sst[:, 2, :], sst[:, 1, :]).then_inc(prec, 1)
                    dve.wait_ge(prec, t + 1)
                    dve.tensor_tensor(se[:], se[:], sst[:, 2, :].unsqueeze(2).to_broadcast([P, HEADS, 64]),
                                      ALU.mult).then_inc(kn_ready, 1)
                if s == 9:
                    for n, (b, p0, np_, cs) in enumerate(((TA, 0, 4, colsum_a), (TB, 4, 2, colsum_b))):
                        dve.wait_ge(kt_done, 2 * t + 1 + n)
                        dve.tensor_reduce(csum[:, p0:p0 + np_, :], b[:, 0:np_ * P].rearrange(
                            "p (h i n) -> p h i n", i=2, n=64), AX, ALU.add).then_inc(cs, 1)
                if s == 10:
                    dve.wait_ge(cst_done, t + 1)
                    dve.tensor_reduce(dmx[:, 0, :], M6[0:HEADS, 0:P].rearrange("p (h n) -> p h n", h=2), AX,
                                      ALU.max).then_inc(dmax, 1)
                    dve.wait_ge(dmax, t + 1)
                    dve.reciprocal(dmx[:, 1, :], dmx[:, 0, :]).then_inc(drec, 1)
                    dve.wait_ge(drec, t + 1)
                    dve.tensor_scalar(dbc[:], dmx[:, 1, :].unsqueeze(2).to_broadcast([HEADS, 2, 64]), -1.0, None,
                                      ALU.mult).then_inc(dbc_ready, 1)
                if s == 11:
                    dve.wait_ge(dbt_done, t + 1)
                    dve.tensor_copy(nid[:].rearrange("p h i -> p (h i)"), M7[:, 0:HEADS]).then_inc(nid_ready, 1)

            def front_last(t):
                dve.wait_ge(nid_ready, t + 1)
                for i in range(2):
                    dve.wait_ge(m0_done, 2 * t + i + 1)
                    dve.tensor_tensor(m0[:, i], (SA, SB_)[i][:, 0:PAIRS * ROW].rearrange("p (h c) -> p h c", c=ROW)[:, :, 0:64],
                                      nid[:, :, i:i + 1].to_broadcast([P, PAIRS, 64]), ALU.mult).then_inc(m0_scaled, 1)
                    dve.wait_ge(m0_scaled, 2 * t + i + 1)
                    for half in range(2 - i):
                        a, z = 64 * half, 64 * half + 64
                        dve.tensor_tensor(r0[a:z, i, :, half, :], m0[a:z, i, :, :],
                                          eye[a:z, :].unsqueeze(1).to_broadcast([64, PAIRS, 64]),
                                          ALU.add).then_inc(r0_ready, 1)

            def newton(k, phase, t):
                src = r0 if k == 0 else rr
                for i in range(2):
                    n = 12 * t + 2 * k + i
                    if phase == 0:
                        dve.wait_ge(q_ready, n + 1)
                        for half in range(2):
                            a, z = 64 * half, 64 * half + 64
                            dve.scalar_tensor_tensor(out=uu[a:z, i, :, half, :], in0=src[a:z, i, :, half, :], scalar=3.0,
                                                     in1=qq[a:z, i], op0=ALU.mult, op1=ALU.add).then_inc(u_ready, 1)
                    elif k == STEPS - 1:
                        dve.wait_ge(prod_done, n + 1)
                        for half in range(2):
                            a, z = 64 * half, 64 * half + 64
                            dve.scalar_tensor_tensor(out=rr[a:z, i, :, half, :], in0=NB[i][a:z], scalar=-0.25,
                                                     in1=eye[a:z, :].unsqueeze(1).to_broadcast([64, PAIRS, 64]),
                                                     op0=ALU.mult, op1=ALU.add).then_inc(r_ready, 1)

            def tail(s, t):
                if s == 1:
                    dve.wait_ge(proj_done, t + 1)
                    dve.wait_ge(res_saved, t + 1)
                    if later(t):
                        dve.wait_ge(h2_saved, t)
                    dve.tensor_tensor(h2[:].unsqueeze(1), M6[:, 0:DIM].unsqueeze(1), acc[:, bass.ds(t, 1), :],
                                      ALU.add).then_inc(h2_ready, 1)
                    dve.wait_ge(h2_ready, t + 1)
                    dve.bn_stats(bn2[:, 0:6], h2[:]).then_inc(tbn_a, 1)
                    wait_first(tbn_a, t + 1)
                    dve.bn_aggr(bn2[:, 6:8], bn2[:, 0:6]).then_inc(tbn_b, 1)
                if s == 3:
                    dve.wait_ge(trstd, RSQ * (t + 1))
                    dve.tensor_scalar(x2[:, 0:DIM], h2[:], bn2[:, 6:7], rst[:, 1:2], ALU.subtract,
                                      ALU.mult).then_inc(x2_ready, 1)
                    dve.tensor_scalar(x2[:, DIM:], h2[:, DA:], bn2[:, 6:7], rst[:, 1:2], ALU.subtract,
                                      ALU.mult).then_inc(x2_ready, 1)
                if s == 5:
                    dve.wait_ge(logits_done, t + 1)
                    dve.tensor_reduce(rst[:, 0:1], SA[:, 0:EXPERTS], AX, ALU.max, negate=True).then_inc(lmax, 1)
                if s == 6:
                    wait_first(lexp, t + 1)
                    dve.max(rt[:, 1, 0:TOPK], rt[:, 0, :]).then_inc(ltop, 1)
                    wait_first(ltop, t + 1)
                    dve.match_replace(rt[:, 2, :], rt[:, 1, 0:TOPK], rt[:, 0, :], -1.0).then_inc(lrep, 1)
                    dve.wait_ge(lrep, t + 1)
                    dve.scalar_tensor_tensor(out=rt[:, 3, :], in0=rt[:, 2, :], scalar=0.0, in1=rt[:, 0, :],
                                             op0=ALU.is_lt, op1=ALU.mult).then_inc(lsel, 1)
                    dve.wait_ge(lsel, t + 1)
                    dve.tensor_reduce(rst[:, 2:3], rt[:, 3, :], AX, ALU.add).then_inc(lsum, 1)
                    dve.wait_ge(lsum, t + 1)
                    dve.reciprocal(rst[:, 3:4], rst[:, 2:3]).then_inc(linv, 1)
                    dve.wait_ge(linv, t + 1)
                    dve.tensor_scalar(comb[:, bass.ds(t, 1), :], rt[:, 3, :].unsqueeze(1), rst[:, 3:4], None,
                                      ALU.mult).then_inc(comb_ready, 1)

            def iteration(t, centre_on=True, front_on=True, tail_on=True):
                for s in range(2 * STEPS):
                    newton(s // 2, s % 2, t)
                    if tail_on:
                        tail(s, t - 1)
                    if front_on:
                        front(s, t + 1)
                    if s == 9 and centre_on:
                        centre(t + 2)
                if front_on:
                    front_last(t + 1)

            dve.memset(scrap[:], 0.0).then_inc(scrap_set, 1)
            dve.wait_ge(scrap_set, 1)
            dve.wait_ge(const_loaded, 16)
            dve.wait_ge(wsh_loaded, 64)
            n = 0
            for f in range(5):
                for c in range(6):
                    hh, ch = divmod(c, 3)
                    g = gbs[:, 0, hh * 15 + 3 * f + ch:hh * 15 + 3 * f + ch + 1]
                    if f == 0:
                        dve.tensor_scalar(weff[:, c, :], wsh[:, hh, f, ch, :], g, None, ALU.mult).then_inc(folded, 1)
                    else:
                        dve.wait_ge(folded, n - 5)
                        dve.scalar_tensor_tensor(out=weff[:, c, :], in0=wsh[:, hh, f, ch, :], scalar=g, in1=weff[:, c, :],
                                                 op0=ALU.mult, op1=ALU.add).then_inc(folded, 1)
                    n += 1
            for c in range(2):
                dve.tensor_scalar(weff[:, 6 + c, :], whalo[:, c, :], gbs[:, 0, 30 + c:31 + c], None,
                                  ALU.mult).then_inc(folded, 1)
            dve.wait_ge(beta_done, 1)
            dve.tensor_copy(crow[:], M6[0:1, 0:DIM]).then_inc(crow_ready, 1)
            dve.wait_ge(cbc_done, 1)
            dve.tensor_tensor(cvec[:], M7[:, 0:DIM], tokb[:], ALU.add).then_inc(cvec_ready, 1)
            dve.wait_ge(cvec_ready, 1)
            centre(0)
            for s in range(2 * STEPS):
                front(s, 0)
                if s == 9:
                    centre(1)
            front_last(0)
            iteration(0, tail_on=False)
            with dve.Fori(1, NT - 2) as t:
                iteration(t)
            iteration(NT - 2, centre_on=False)
            iteration(NT - 1, centre_on=False, front_on=False)
            for s in range(2 * STEPS):
                tail(s, NT - 1)

            dve.wait_ge(comb_ready, NT)
            dve.wait_ge(h2_saved, NT)
            dve.wait_ge(ffw_loaded, 64)
            dve.tensor_copy(scrap[:, 0:1], scrap[:, 1:2]).then_inc(expert_added, 1)
            dve.tensor_copy(scrap[:, 2:3], scrap[:, 1:2]).then_inc(expert_added, 1)
            with dve.Fori(0, NT // GT) as g:
                def low_part(c):
                    dve.wait_ge(whi_ready, (g * HID + c + 1) * 2)
                    k = c % 3
                    for w, high, raw, a in ((wal, wah, w1_a, 0), (wb, wb, w1_b, 64)):
                        dve.tensor_tensor(w[a:P, k, :], raw[a:P, c * P:(c + 1) * P], high[a:P, k, :].bitcast(F32),
                                          ALU.subtract).then_inc(wlo_ready, 1)
                low_part(0)
                low_part(1)
                c = 0
                for e in range(EXPERTS):
                    for _ in range(WIDTH[e]):
                        if c + 2 < HID:
                            low_part(c + 2)
                        c += 1
                    dve.wait_ge(down_done, g * EXPERTS + e + 1)
                    dve.wait_ge(expert_added, g * EXPERTS + e + 2)
                    for j in range(GT):
                        a = acc[:, bass.ds(g * GT + j, 1), :]
                        last = dve.scalar_tensor_tensor(
                            out=a, in0=ps[:, 2 + 2 * (e % 2) + j // 2, (j % 2) * DIM:(j % 2 + 1) * DIM].unsqueeze(1),
                            scalar=comb[:, bass.ds(g * GT + j, 1), e:e + 1].rearrange("p a b -> p (a b)"), in1=a,
                            op0=ALU.mult, op1=ALU.add)
                    last.then_inc(expert_added, 1)


def kernel(x, L0_tok_gamma, L0_tok_beta, L0_tok_W, L0_tok_b, L0_attn_w_qkv, L0_attn_w_proj, L0_attn_b_proj,
           L0_ffn_router_w, L0_ffn_w1, L0_ffn_w2):
    import numpy as np
    import concourse.bacc as bacc
    from concourse.bass_utils import run_bass_kernel_spmd

    x = np.asarray(x)
    pad = np.zeros((IMGS, 130, 130, 3), x.dtype)
    pad[:, 1:129, 1:129] = x
    def rows_of(a, first):
        return a[:, first:first + 113:16]
    inner = np.ascontiguousarray(pad[:, 1:129, 1:129]).reshape(IMGS, 8, 2, 8, 8, 16, 3)
    inner = inner.transpose(0, 1, 4, 2, 6, 3, 5).reshape(IMGS * TOK, 768)
    side = np.stack([pad[:, 1:129, 0:113:16], pad[:, 1:129, 17:130:16]], 3)
    side = side.reshape(IMGS, 8, 16, 8, 2, 3).transpose(0, 1, 3, 2, 4, 5).reshape(IMGS * TOK, 96)
    ends = np.stack([rows_of(pad, 0), rows_of(pad, 17)], 2)[:, :, :, 1:129]
    ends = ends.reshape(IMGS, 8, 2, 8, 16, 3).transpose(0, 1, 3, 2, 4, 5).reshape(IMGS * TOK, 96)
    gap = np.zeros((IMGS * TOK, 32), x.dtype)
    xw = np.concatenate([inner, side, gap, ends, gap], 1).reshape(NT, P, CH * P)

    def by_pixel(a):
        a = np.asarray(a).reshape(16, 16, 5, 3, -1)
        z = np.zeros_like(a)
        z[:, :, 0] = a[:, :, 0]
        z[:, :15, 1] = a[:, 1:, 1]
        z[:, 1:, 2] = a[:, :15, 2]
        z[:15, :, 3] = a[1:, :, 3]
        z[1:, :, 4] = a[:15, :, 4]
        inside = z.reshape(2, P, 5, 3, -1).transpose(1, 0, 2, 3, 4)
        border = np.zeros((P, 2, a.shape[-1]), a.dtype)
        border[:96, 0] = np.stack([a[:, 0, 1], a[:, 15, 2]], 1).reshape(96, -1)
        border[:96, 1] = np.stack([a[0, :, 3], a[15, :, 4]], 0).reshape(96, -1)
        return inside, border

    wsh, whalo = by_pixel(L0_tok_W)
    gs, gh = by_pixel(L0_tok_gamma)
    bs, bh = by_pixel(L0_tok_beta)
    gb = np.stack([np.concatenate([gs.reshape(P, 30), gh[:, :, 0]], 1),
                   np.concatenate([bs.reshape(P, 30), bh[:, :, 0]], 1)], 1)

    wt = np.asarray(L0_attn_w_qkv).T
    wqk = wt[:, :2 * DIM]
    wv = wt[:, 2 * DIM:].reshape(DIM, PAIRS, 2, HD).transpose(0, 2, 1, 3).reshape(DIM, DIM)
    pt = np.asarray(L0_attn_w_proj).T.reshape(PAIRS, 2, HD, DIM)
    wp = np.zeros((4, 32, 4, DIM), pt.dtype)
    for p in range(PAIRS):
        for half in range(2):
            wp[p % 4, :HD, 2 * (p // 4) + half] = pt[p, half]

    const = np.zeros((P, C_ALL), np.float32)
    const[:, C_ID:C_ID + P] = np.eye(P)
    const[:, C_EYE:C_EYE + 64] = np.tile(np.eye(64), (2, 1))
    for p in range(P):
        const[p, C_HM + p // HD] = 1
        if p < DB:
            const[p, C_HM + 8 + p // HD] = 1
    const[:, C_PC:C_PC + 8] = [1 / FEAT, 1e-3, 1, 1e-5, -0.5, 1.5, 0, 0]
    copies = np.ones((16, 16), np.float32)
    copies[:, :15] += 1
    copies[:, 1:] += 1
    copies[:15] += 1
    copies[1:] += 1
    const[:, C_MULT:C_MULT + 768] = np.repeat(copies.reshape(2, 1, P), 3, 1).reshape(-1)
    const[:, C_MULT + 768:C_MULT + 864] = 1
    const[:, C_MULT + 896:C_MULT + 992] = 1

    arrays = {
        "x_dram": xw, "ws_dram": wsh, "wh_dram": whalo, "gb_dram": gb, "tb_dram": L0_tok_b,
        "wqk_dram": wqk, "wv_dram": wv, "wp_dram": wp.reshape(P, 4, DIM), "bp_dram": L0_attn_b_proj,
        "rw_dram": np.asarray(L0_ffn_router_w).T, "w1_dram": L0_ffn_w1, "w2_dram": L0_ffn_w2, "const_dram": const,
    }
    arrays = {k: np.ascontiguousarray(v) for k, v in arrays.items()}
    nc = bacc.Bacc("TRN2", target_bir_lowering=False, num_devices=1)
    args = [nc.dram_tensor(k, v.shape, mybir.dt.from_np(v.dtype), kind="ExternalInput").ap() for k, v in arrays.items()]
    args.append(nc.dram_tensor("out_dram", (NT, P, DIM), F32, kind="ExternalOutput").ap())
    vit_block_kernel(nc, *args)
    r = run_bass_kernel_spmd(nc, [arrays], core_ids=[0])
    return np.asarray(r.results[0]["out_dram"]).reshape(IMGS, TOK, DIM)
```

```python
from contextlib import ExitStack

import concourse.bass as bass
from concourse import mybir

P = 128
IMGS, TOK, DIM = 32, 64, 192
HEADS, HD = 12, 16
PAIRS = HEADS // 2
NT = IMGS * TOK // P
FEAT = 3840
CH = 8
DA, DB = 128, DIM - 128
STEPS = 6
EXPERTS, TOPK = 16, 8
WIDTH = [1] * 8 + [2] * 8
HID = sum(WIDTH)
RSQ = 16
LN_RSQ = RSQ - 1
GT = 4
ROW = 80

F32 = mybir.dt.float32
I32 = mybir.dt.int32
F32R = mybir.dt.float32r
ALU = mybir.AluOpType
ACT = mybir.ActivationFunctionType
AX = mybir.AxisListType.X

C_ID, C_EYE, C_HM, C_PC, C_MULT = 0, 128, 192, 204, 212
C_ALL = C_MULT + CH * P


def later(t):
    return not isinstance(t, int) or t > 0


def vit_block_kernel(nc, x, ws, wh, gb, tok_b, wqk, wv, wp, bp, rw, w1, w2, const, out):
    with ExitStack() as ctx:
        def sb(name, shape, dtype=F32):
            return ctx.enter_context(nc.sbuf_tensor(name, shape, dtype))

        def sem(name):
            return ctx.enter_context(nc.semaphore(name))

        cst = sb("cst", [P, C_ALL])
        ident = cst[:, C_ID:C_ID + P]
        eye = cst[:, C_EYE:C_EYE + 64]
        head_mask = cst[:, C_HM:C_HM + HEADS]
        pc = cst[:, C_PC:C_PC + 8]
        mult = cst[:, C_MULT:C_MULT + CH * P]
        wsh = sb("wsh", [P, 2, 5, 3, DIM])
        whalo = sb("whalo", [P, 2, DIM])
        gbs = sb("gbs", [P, 2, 32])
        weff = sb("weff", [P, CH, DIM])
        crow = sb("crow", [1, DIM])
        ones = sb("ones", [1, P])
        tokb = sb("tokb", [P, DIM])
        cvec = sb("cvec", [P, DIM])
        wqk_a, wqk_b = sb("wqk_a", [DA, 2 * DIM]), sb("wqk_b", [DB, 2 * DIM])
        wv_a, wv_b = sb("wv_a", [DA, DIM]), sb("wv_b", [DB, DIM])
        wp_sb = sb("wp_sb", [P, 4, DIM])
        bp_sb = sb("bp_sb", [P, DIM])
        rw_a, rw_b = sb("rw_a", [DA, EXPERTS]), sb("rw_b", [DB, EXPERTS])
        w1_a, w1_b = sb("w1_a", [DA, HID * P]), sb("w1_b", [P, HID * P])
        w2_sb = sb("w2_sb", [P, HID, DIM])

        work = sb("work", [P, 2 * CH * P])
        xin = work[:, 0:CH * P]
        xc = work[:, CH * P:].rearrange("p (c n) -> p c n", n=P)
        sq = sb("sq", [P, CH * P])
        xct = sb("xct", [P, CH, P])
        scrap = sb("scrap", [P, 4])
        st = sb("st", [P, 24])
        h_t = sb("h_t", [P, DIM])
        xl = sb("xl", [P, DIM])
        xlt = sb("xlt", [P, 2, P])
        bn = sb("bn", [P, 8])
        qt = sb("qt", [P, 2, P])
        kb_a = sb("kb_a", [P, 2, 8, 64])
        kb_b = sb("kb_b", [DB, 2, 4, 64])
        se = sb("se", [P, HEADS, 64])
        sst = sb("sst", [P, 3, HEADS])
        kv = sb("kv", [P, 2, PAIRS, 2, ROW])
        csum = sb("csum", [P, PAIRS, 2])
        dmx = sb("dmx", [HEADS, 2, 2])
        dbc = sb("dbc", [HEADS, 2, 64])
        nid = sb("nid", [P, PAIRS, 2])
        m0 = sb("m0", [P, 2, PAIRS, 64])
        r0 = sb("r0", [P, 2, PAIRS, 2, 64])
        rr = sb("rr", [P, 2, PAIRS, 2, 64])
        uu = sb("uu", [P, 2, PAIRS, 2, 64])
        qq = sb("qq", [P, 2, PAIRS, 64])
        y_t = sb("y_t", [P, 2, PAIRS, 32])
        ot = sb("ot", [P, 2, 2, P])
        h2 = sb("h2", [P, DIM])
        x2 = sb("x2", [P, 2 * P])
        x2t = sb("x2t", [P, 2, P])
        bn2 = sb("bn2", [P, 8])
        rt = sb("rt", [P, 4, EXPERTS])
        rst = sb("rst", [P, 12])
        acc = sb("acc", [P, NT, DIM])
        comb = sb("comb", [P, NT, EXPERTS])
        xhi, xlo = sb("xhi", [P, 2, NT * P], F32R), sb("xlo", [P, 2, NT * P], F32R)
        hid = work[:].rearrange("p (c n) -> p c n", c=4)
        wah, wal, wb = (sb(n, [P, 3, P], F32R) for n in ("wah", "wal", "wb"))

        ps = ctx.enter_context(nc.psum_tensor("ps", [P, 8, 512], F32))
        NB = [ps[:, i, 0:PAIRS * 64].rearrange("p (h n) -> p h n", h=PAIRS) for i in (0, 1)]
        SA, SB_, TA, TB, M6, M7 = (ps[:, i, :] for i in (2, 3, 4, 5, 6, 7))

        def sems(names):
            return [sem(n) for n in names.split()]

        const_loaded, wsh_top_loaded, wsh_loaded, x_loaded = sems("const_loaded wsh_top_loaded wsh_loaded x_loaded")
        attw_loaded, ffw_loaded, x_free, ones_set = sems("attw_loaded ffw_loaded x_free ones_set")
        scrap_set, zeros_set, folded, beta_done = sems("scrap_set zeros_set folded beta_done")
        crow_ready, cbc_done, cvec_ready, xmean = sems("crow_ready cbc_done cvec_ready xmean")
        xmean2, xc_ready, sq_ready, xvar, xrstd = sems("xmean2 xc_ready sq_ready xvar xrstd")
        xtr_done, xct_ready, tok_done, h_ready = sems("xtr_done xct_ready tok_done h_ready")
        res_saved, bn_a, bn_b, lrstd, xl_ready = sems("res_saved bn_a bn_b lrstd xl_ready")
        xltr_done, xlt_ready, qk_done, q_copied = sems("xltr_done xlt_ready qk_done q_copied")
        kb_ready, v_done, v_copied, scores_done, smax = sems("kb_ready v_done v_copied scores_done smax")
        sdiff, probs_exp, psumd, prec, kn_ready = sems("sdiff probs_exp psumd prec kn_ready")
        kt_done, colsum_a, colsum_b, kt_copied = sems("kt_done colsum_a colsum_b kt_copied")
        cst_done, dmax, drec, dbc_ready, dbt_done = sems("cst_done dmax drec dbc_ready dbt_done")
        nid_ready, m0_done, m0_scaled, r0_ready = sems("nid_ready m0_done m0_scaled r0_ready")
        r0_last_ready, y_copied, square_done = sems("r0_last_ready y_copied square_done")
        q_ready, u_ready, prod_done, r_ready, o_done = sems("q_ready u_ready prod_done r_ready o_done")
        o_copied, proj_done, h2_ready, h2_saved = sems("o_copied proj_done h2_ready h2_saved")
        tbn_a, tbn_b, trstd, x2_ready, x2tr_done = sems("tbn_a tbn_b trstd x2_ready x2tr_done")
        x2t_ready, xhi_ready, x2_saved, logits_done = sems("x2t_ready xhi_ready x2_saved logits_done")
        lmax, lexp, ltop, lrep, lsel, lsum, linv = sems("lmax lexp ltop lrep lsel lsum linv")
        comb_ready, whi_ready, wlo_ready, up_done = sems("comb_ready whi_ready wlo_ready up_done")
        gelu_done, down_done, expert_added = sems("gelu_done down_done expert_added")
        out_stored, = sems("out_stored")
        block = ctx.enter_context(nc.Block())

        def wait_first(semaphore, value):
            nc.vector.wait_ge(semaphore, value)
            nc.vector.tensor_copy(scrap[:, 0:1], scrap[:, 1:2])

        @block.sync
        def _(sp):
            sp.dma_start(cst[:], const).then_inc(const_loaded, 16)
            sp.dma_start(xin, x[0]).then_inc(x_loaded, 16)
            sp.dma_start(gbs[:], gb).then_inc(wsh_top_loaded, 16)
            sp.dma_start(wsh[:, 0], ws[:, 0]).then_inc(wsh_top_loaded, 16)
            sp.dma_start(wsh[:, 1], ws[:, 1]).then_inc(wsh_loaded, 16)
            sp.dma_start(whalo[:], wh).then_inc(wsh_loaded, 16)
            sp.dma_start(tokb[:], tok_b.partition_broadcast(P)).then_inc(wsh_loaded, 16)
            sp.dma_start(wqk_a[:], wqk[0:DA, :]).then_inc(attw_loaded, 16)
            sp.dma_start(wqk_b[:], wqk[DA:DIM, :]).then_inc(attw_loaded, 16)
            sp.dma_start(wv_a[:], wv[0:DA, :]).then_inc(attw_loaded, 16)
            sp.dma_start(wv_b[:], wv[DA:DIM, :]).then_inc(attw_loaded, 16)
            sp.dma_start(wp_sb[:], wp).then_inc(attw_loaded, 16)
            sp.dma_start(bp_sb[:], bp.partition_broadcast(P)).then_inc(attw_loaded, 16)
            sp.dma_start(rw_a[:], rw[0:DA, :]).then_inc(attw_loaded, 16)
            sp.dma_start(rw_b[:], rw[DA:DIM, :]).then_inc(attw_loaded, 16)
            sp.wait_ge(x_free, 1)
            sp.dma_start(xin, x[1]).then_inc(x_loaded, 16)
            sp.dma_start(w1_a[:], w1[0:DA, :]).then_inc(ffw_loaded, 16)
            sp.dma_start(w1_b[0:DB, :], w1[DA:DIM, :]).then_inc(ffw_loaded, 16)
            sp.dma_start(w1_b[DB:P, :], w1[DA:DIM, :]).then_inc(ffw_loaded, 16)
            sp.dma_start(w2_sb[:], w2.rearrange("(c p) n -> p c n", p=P)).then_inc(ffw_loaded, 16)
            with sp.Fori(2, NT) as t:
                sp.wait_ge(x_free, t)
                sp.dma_start(xin, x[bass.ds(t, 1)].rearrange("a p f -> (a p) f")).then_inc(x_loaded, 16)
            with sp.Fori(0, NT // GT) as g:
                sp.wait_ge(expert_added, (g + 1) * EXPERTS + 2)
                sp.dma_start(out[bass.ds(g * GT, GT)].rearrange("t p n -> p t n"),
                             acc[:, bass.ds(g * GT, GT), :]).then_inc(out_stored, 16)
            sp.wait_ge(out_stored, 16 * (NT // GT))

        @block.gpsimd
        def _(pool):
            pool.memset(ones[:], 1.0).then_inc(ones_set, 1)
            for buf in (r0, rr, uu, kv, y_t):
                pool.memset(buf[:], 0.0).then_inc(zeros_set, 1)

            def front_last(t):
                pool.wait_ge(m0_scaled, 2 * t + 2)
                pool.tensor_tensor(r0[64:P, 1, :, 1, :], m0[64:P, 1, :, :],
                                   eye[64:P, :].unsqueeze(1).to_broadcast([64, PAIRS, 64]),
                                   ALU.add).then_inc(r0_last_ready, 1)

            def rsqrt(out_, var, scaled, w, steps, t):
                n = [t * (RSQ if scaled else LN_RSQ)]

                def step(op, wait=True):
                    op.then_inc(steps, 1)
                    n[0] = n[0] + 1
                    if wait:
                        pool.wait_ge(steps, n[0])
                v, hv, a, y = (w[:, k:k + 1] for k in range(4))
                if scaled:
                    step(pool.tensor_tensor(v, var, pc[:, 0:1], ALU.mult))
                    step(pool.tensor_tensor(v, v, pc[:, 1:2], ALU.add))
                else:
                    step(pool.tensor_tensor(v, var, pc[:, 3:4], ALU.add))
                step(pool.tensor_tensor(hv, v, pc[:, 4:5], ALU.mult), wait=False)
                step(pool.tensor_scalar(y.bitcast(I32), v.bitcast(I32), -0.5, float(0x5f3759df), ALU.mult, ALU.add))
                for k in range(3):
                    step(pool.tensor_tensor(a, y, y, ALU.mult))
                    step(pool.tensor_tensor(a, a, hv, ALU.mult))
                    step(pool.tensor_tensor(a, a, pc[:, 5:6], ALU.add))
                    step(pool.tensor_tensor(out_ if k == 2 else y, a, y, ALU.mult))

            def token_rstd(t):
                pool.wait_ge(xvar, t + 1)
                rsqrt(st[:, 4:5], st[:, 2:3], True, st[:, 8:13], xrstd, t)

            def ln1_rstd(t):
                pool.wait_ge(bn_b, t + 1)
                rsqrt(st[:, 5:6], bn[:, 7:8], False, st[:, 16:21], lrstd, t)

            def tail(t):
                pool.wait_ge(tbn_b, t + 1)
                rsqrt(rst[:, 1:2], bn2[:, 7:8], False, rst[:, 4:9], trstd, t)

            def saves(t):
                pool.wait_ge(h2_ready, t + 1)
                pool.tensor_copy(acc[:, bass.ds(t, 1), :], h2[:].unsqueeze(1)).then_inc(h2_saved, 1)
                pool.wait_ge(xhi_ready, t + 1)
                pool.tensor_tensor(xlo[:, :, bass.ds(t * P, P)], x2t[:], xhi[:, :, bass.ds(t * P, P)].bitcast(F32),
                                   ALU.subtract).then_inc(x2_saved, 1)

            def iteration(t, centre_on=True, front_on=True, tail_on=True):
                pool.wait_ge(r0_last_ready, t + 1)
                if tail_on:
                    tail(t - 1)
                if front_on:
                    ln1_rstd(t + 1)
                if tail_on:
                    saves(t - 1)
                    pool.wait_ge(x2_saved, t)
                if centre_on:
                    token_rstd(t + 2)
                    pool.wait_ge(xrstd, RSQ * (t + 3))
                if front_on:
                    front_last(t + 1)

            pool.wait_ge(const_loaded, 16)
            pool.wait_ge(zeros_set, 5)
            token_rstd(0)
            ln1_rstd(0)
            token_rstd(1)
            pool.wait_ge(xrstd, RSQ * 2)
            front_last(0)
            iteration(0, tail_on=False)
            with pool.Fori(1, NT - 2) as t:
                iteration(t)
            iteration(NT - 2, centre_on=False)
            iteration(NT - 1, centre_on=False, front_on=False)
            tail(NT - 1)
            saves(NT - 1)

        @block.tensor
        def _(pe):
            def front(s, t):
                if s == 0:
                    pe.wait_ge(xc_ready, t + 1)
                    if later(t):
                        pe.wait_ge(kt_copied, 4 * t)
                    for c in range(CH):
                        last = pe.transpose((TA, TB)[c // 4][:, (c % 4) * P:(c % 4 + 1) * P], xc[:, c, :], ident)
                        if c % 4 == 3:
                            last.then_inc(xtr_done, 1)
                if s == 1:
                    pe.wait_ge(xct_ready, 2 * t + 2)
                    for c in range(CH):
                        last = pe.matmul(M7[:, 0:DIM], xct[:, c, :], weff[:, c, :], start=(c == 0), stop=(c == CH - 1))
                    last.then_inc(tok_done, 1)
                if s == 4:
                    pe.wait_ge(xl_ready, t + 1)
                    pe.transpose(M6[:, 0:P], xl[:, 0:DA], ident)
                    pe.transpose(M6[0:DB, P:2 * P], xl[:, DA:DIM], ident).then_inc(xltr_done, 1)
                if s == 5:
                    pe.wait_ge(xlt_ready, 2 * t + 2)
                    for n, (c0, m) in enumerate(((0, DA), (DA, DB), (DIM, DA), (DIM + DA, DB))):
                        pe.matmul(M7[0:m, n * P:(n + 1) * P], wqk_a[:, c0:c0 + m], xlt[:, 0, :], start=True, stop=False)
                        last = pe.matmul(M7[0:m, n * P:(n + 1) * P], wqk_b[:, c0:c0 + m], xlt[0:DB, 1, :],
                                         start=False, stop=True)
                    last.then_inc(qk_done, 1)
                if s == 6:
                    pe.matmul(M6[:, 0:DIM], xlt[:, 0, :], wv_a[:], start=True, stop=False)
                    pe.matmul(M6[:, 0:DIM], xlt[0:DB, 1, :], wv_b[:], start=False, stop=True).then_inc(v_done, 1)
                if s == 7:
                    pe.wait_ge(q_copied, 2 * t + 2)
                    pe.wait_ge(kb_ready, 4 * t + 4)
                    for i in range(2):
                        r = slice(64 * i, 64 * i + 64)
                        pe.matmul(SA[r, :], qt[:, 0, r], kb_a[:, i].rearrange("p h n -> p (h n)"), start=True, stop=True)
                        last = pe.matmul(SB_[r, 0:256], qt[0:DB, 1, r], kb_b[:, i].rearrange("p h n -> p (h n)"),
                                         start=True, stop=True)
                    last.then_inc(scores_done, 1)
                if s == 10:
                    pe.wait_ge(kn_ready, t + 1)
                    for p in range(PAIRS):
                        last = pe.transpose((TA, TB)[p // 4][:, (p % 4) * P:(p % 4 + 1) * P],
                                            se[:, 2 * p:2 * p + 2, :].rearrange("p h n -> p (h n)"), ident)
                        if p in (3, PAIRS - 1):
                            last.then_inc(kt_done, 1)
                if s == 11:
                    pe.wait_ge(colsum_a, t + 1)
                    pe.wait_ge(colsum_b, t + 1)
                    pe.wait_ge(v_copied, 4 * t + 4)
                    pe.transpose(M6[0:HEADS, 0:P], csum[:].rearrange("p h i -> p (h i)"), ident).then_inc(cst_done, 1)

            def front_last(t):
                pe.wait_ge(kt_copied, 4 * t + 4)
                pe.wait_ge(sdiff, 2 * t + 2)
                for i in range(2):
                    for p in range(PAIRS):
                        if (i, p) == (1, 2):
                            pe.wait_ge(dbc_ready, t + 1)
                            pe.matmul(M7[:, 0:HEADS], dbc[:].rearrange("p h n -> p (h n)"), ident[0:HEADS, 0:HEADS],
                                      start=True, stop=True).then_inc(dbt_done, 1)
                        for half in range(2):
                            r = slice(64 * half, 64 * half + 64)
                            last = pe.matmul((SA, SB_)[i][r, p * ROW:(p + 1) * ROW], kv[:, i, p, half, 0:64],
                                             kv[:, i, p, half, :], start=True, stop=True)
                    last.then_inc(m0_done, 1)

            def newton(k, phase, t):
                for i in range(2):
                    n = 12 * t + 2 * k + i
                    src = r0 if k == 0 else rr
                    for half in range(2):
                        r = slice(64 * half, 64 * half + 64)
                        if phase == 0:
                            if k > 0:
                                pe.wait_ge(r_ready, 2 * n - 3 + half)
                            elif i == half == 1:
                                pe.wait_ge(r0_last_ready, t + 1)
                            else:
                                pe.wait_ge(r0_ready, 3 * t + 2 * i + half + 1)
                        else:
                            pe.wait_ge(u_ready, 2 * n + half + 1)
                        for p in range(PAIRS):
                            lhs = src[:, i, p, half, :] if phase == 0 else qq[:, i, p, :]
                            rhs = src[:, i, p, half, :] if phase == 0 else uu[:, i, p, half, :]
                            last = pe.matmul(NB[i][r, p, :], lhs, rhs, start=True, stop=True)
                    last.then_inc((square_done, prod_done)[phase], 1)

            def tail(s, t):
                if s == 0:
                    pe.wait_ge(r_ready, 24 * t + 24)
                    pe.wait_ge(y_copied, 2 * t + 2)
                    for i in range(2):
                        for p in range(PAIRS):
                            g, j = divmod(p, 4)
                            o = M7[32 * j:32 * j + 32, g * 256:(g + 1) * 256].rearrange("p (h i n) -> p h i n", h=2, i=2)
                            last = pe.matmul(o[:, :, i, :], y_t[:, i, p, :], rr[:, i, p].rearrange("p h n -> p (h n)"),
                                             start=True, stop=True, tile_position=(0, 32 * j))
                    last.then_inc(o_done, 1)
                if s == 1:
                    pe.wait_ge(o_copied, 2 * t + 2)
                    for g in range(2):
                        rows = P if g == 0 else 64
                        for half in range(2):
                            last = pe.matmul(M6[:, 0:DIM], ot[0:rows, g, half, :], wp_sb[0:rows, 2 * g + half, :],
                                             start=(g + half == 0), stop=(g + half == 2))
                    last.then_inc(proj_done, 1)
                if s == 4:
                    pe.wait_ge(x2_ready, 2 * t + 2)
                    pe.transpose(M7[:, 0:P], x2[:, 0:DA], ident)
                    pe.transpose(M7[:, P:2 * P], x2[:, DA:], ident).then_inc(x2tr_done, 1)
                if s == 5:
                    pe.wait_ge(x2t_ready, t + 1)
                    pe.matmul(SA[:, 0:EXPERTS], x2t[:, 0, :], rw_a[:], start=True, stop=False)
                    pe.matmul(SA[:, 0:EXPERTS], x2t[0:DB, 1, :], rw_b[:], start=False, stop=True).then_inc(logits_done, 1)

            def bank_waits(s, t, front_on, tail_on):
                if s == 0 and tail_on:
                    pe.wait_ge(nid_ready, t + 1)
                if s == 4 and front_on and tail_on:
                    pe.wait_ge(h2_ready, t)
                if s == 4 and tail_on and front_on:
                    pe.wait_ge(h_ready, t + 2)
                if s == 5 and tail_on and front_on:
                    pe.wait_ge(xhi_ready, t)
                if s == 7 and tail_on and front_on:
                    pe.wait_ge(lexp, t)

            def iteration(t, front_on=True, tail_on=True):
                for s in range(2 * STEPS):
                    if s > 0:
                        newton(s // 2, s % 2, t)
                    if s == 5:
                        pe.wait_ge(y_copied, 2 * t + 2)
                    if s == 1 and front_on and tail_on:
                        pe.wait_ge(o_copied, 2 * t)
                    if tail_on:
                        bank_waits(s, t, front_on, tail_on)
                        tail(s, t - 1)
                    if front_on:
                        front(s, t + 1)
                    if s == 0:
                        newton(0, 0, t)
                if front_on:
                    front_last(t + 1)

            pe.wait_ge(const_loaded, 16)
            front(0, 0)
            n = 0
            for hh in range(2):
                if hh == 0:
                    pe.wait_ge(wsh_top_loaded, 32)
                else:
                    pe.wait_ge(wsh_loaded, 48)
                for f in range(15):
                    pe.matmul(M6[0:1, 0:DIM], gbs[:, 1, hh * 15 + f:hh * 15 + f + 1], wsh[:, hh, f // 3, f % 3, :],
                              start=(n == 0), stop=False)
                    n += 1
            pe.matmul(M6[0:1, 0:DIM], gbs[:, 1, 30:31], whalo[:, 0, :], start=False, stop=False)
            pe.matmul(M6[0:1, 0:DIM], gbs[:, 1, 31:32], whalo[:, 1, :], start=False, stop=True).then_inc(beta_done, 1)
            pe.wait_ge(crow_ready, 1)
            pe.wait_ge(ones_set, 1)
            pe.matmul(M7[:, 0:DIM], ones[:], crow[:], start=True, stop=True).then_inc(cbc_done, 1)
            pe.wait_ge(cvec_ready, 1)
            pe.wait_ge(folded, 32)
            pe.wait_ge(attw_loaded, 16 * 8)
            for s in range(1, 2 * STEPS):
                front(s, 0)
            front_last(0)
            iteration(0, tail_on=False)
            with pe.Fori(1, NT - 1) as t:
                iteration(t)
            iteration(NT - 1, front_on=False)
            for s in range(2 * STEPS):
                tail(s, NT - 1)

            pe.wait_ge(ffw_loaded, 64)
            pe.wait_ge(x2_saved, NT)
            pe.wait_ge(lexp, NT)
            first = [sum(WIDTH[:e]) for e in range(EXPERTS)]
            with pe.Fori(0, NT // GT) as g:
                def up(c):
                    pe.wait_ge(whi_ready, (g * HID + c + 1) * 2)
                    pe.wait_ge(wlo_ready, (g * HID + c + 1) * 2)
                    if c >= 2:
                        pe.wait_ge(gelu_done, g * HID + (c - 1))
                    tok = bass.ds(g * GT * P, GT * P)
                    k = c % 3
                    parts = ((wah, xhi, 0), (wah, xlo, 0), (wal, xhi, 0), (wb, xhi, 1), (wb, xlo, 1))
                    for n, (w, xs, half) in enumerate(parts):
                        last = pe.matmul(ps[:, c % 2, :], w[:, k, :], xs[:, half, tok], start=(n == 0), stop=(n == 4))
                    last.then_inc(up_done, 1)

                def down(e, c):
                    if c == first[e]:
                        pe.wait_ge(expert_added, g * EXPERTS + e + 1)
                    pe.wait_ge(gelu_done, g * HID + c + 1)
                    for j in range(GT):
                        last = pe.matmul(ps[:, 2 + 2 * (e % 2) + j // 2, (j % 2) * DIM:(j % 2 + 1) * DIM],
                                         hid[:, c % 4, j * P:(j + 1) * P], w2_sb[:, c, :],
                                         start=(c == first[e] and j % 2 == 0), stop=(c == first[e] + WIDTH[e] - 1),
                                         skip_group_check=True)
                    if c == first[e] + WIDTH[e] - 1:
                        last.then_inc(down_done, 1)
                chunks = [(e, first[e] + w) for e in range(EXPERTS) for w in range(WIDTH[e])]
                up(0)
                for e, c in chunks:
                    if c + 1 < HID:
                        up(c + 1)
                    down(e, c)

        @block.scalar
        def _(act):
            def squares(t):
                act.wait_ge(xc_ready, t + 1)
                act.activation(sq[:], xc.rearrange("p c n -> p (c n)"), ACT.Square).then_inc(sq_ready, 1)

            def front(s, t):
                if s == 0:
                    for n, b in enumerate((TA, TB)):
                        act.wait_ge(xtr_done, 2 * t + n + 1)
                        act.activation(xct[:, 4 * n:4 * n + 4, :].rearrange("p c n -> p (c n)"), b,
                                       ACT.Copy).then_inc(xct_ready, 1)
                if s == 4:
                    act.wait_ge(xltr_done, t + 1)
                    act.activation(xlt[:, 0, :], M6[:, 0:P], ACT.Copy).then_inc(xlt_ready, 1)
                    act.activation(xlt[0:DB, 1, :], M6[0:DB, P:2 * P], ACT.Copy).then_inc(xlt_ready, 1)
                if s == 5:
                    act.wait_ge(qk_done, t + 1)
                    act.activation(qt[:, 0, :], M7[:, 0:P], ACT.Copy).then_inc(q_copied, 1)
                    act.activation(qt[0:DB, 1, :], M7[0:DB, P:2 * P], ACT.Copy).then_inc(q_copied, 1)
                if s == 6:
                    act.wait_ge(v_done, t + 1)
                    for i in range(2):
                        for half in range(2):
                            act.activation(kv[64 * half:64 * half + 64, i, :, half, 64:ROW],
                                           M6[64 * i:64 * i + 64, half * 96:half * 96 + 96].rearrange(
                                               "p (h d) -> p h d", d=HD), ACT.Copy).then_inc(v_copied, 1)
                if s == 8:
                    act.wait_ge(sdiff, 2 * t + 2)
                    act.activation(se[:], se[:], ACT.Exp, scale=1.0 / (HD ** 0.5)).then_inc(probs_exp, 1)
                if s == 10:
                    for n, (b, p0, np_) in enumerate(((TA, 0, 4), (TB, 4, 2))):
                        if n == 0:
                            act.wait_ge(kt_done, 2 * t + 1)
                        else:
                            act.wait_ge(colsum_b, t + 1)
                        for half in range(2):
                            a, z = 64 * half, 64 * half + 64
                            act.activation(kv[a:z, :, p0:p0 + np_, half, 0:64].rearrange("p i h n -> p h i n"),
                                           b[a:z, 0:np_ * P].rearrange("p (h i n) -> p h i n", i=2, n=64),
                                           ACT.Copy).then_inc(kt_copied, 1)

            def save_y(t):
                if later(t):
                    act.wait_ge(o_done, t)
                for i in range(2):
                    act.wait_ge(m0_scaled, 2 * t + i + 1)
                    act.activation(y_t[:, i, :, 0:HD],
                                   (SA, SB_)[i][:, 0:PAIRS * ROW].rearrange("p (h c) -> p h c", c=ROW)[:, :, 64:ROW],
                                   ACT.Copy).then_inc(y_copied, 1)

            def newton(k, phase, t):
                for i in range(2):
                    n = 12 * t + 2 * k + i
                    if phase == 0:
                        act.wait_ge(square_done, n + 1)
                        act.activation(qq[:, i], NB[i], ACT.Copy).then_inc(q_ready, 1)
                    elif k < STEPS - 1:
                        act.wait_ge(prod_done, n + 1)
                        for half in range(2):
                            a, z = 64 * half, 64 * half + 64
                            act.activation(rr[a:z, i, :, half, :], NB[i][a:z], ACT.Copy, scale=0.25).then_inc(r_ready, 1)

            def tail(s, t):
                if s == 0:
                    act.wait_ge(o_done, t + 1)
                    act.activation(ot[:, 0].rearrange("p h n -> p (h n)"), M7[:, 0:256], ACT.Copy).then_inc(o_copied, 1)
                    act.activation(ot[0:64, 1].rearrange("p h n -> p (h n)"), M7[0:64, 256:512],
                                   ACT.Copy).then_inc(o_copied, 1)
                if s == 4:
                    act.wait_ge(x2tr_done, t + 1)
                    if later(t):
                        act.wait_ge(x2_saved, t)
                    m7 = M7[:, 0:2 * P].rearrange("p (a n) -> p a n", a=2)
                    act.activation(x2t[:], m7, ACT.Copy).then_inc(x2t_ready, 1)
                    act.activation(xhi[:, :, bass.ds(t * P, P)], m7, ACT.Copy).then_inc(xhi_ready, 1)
                if s == 5:
                    act.wait_ge(lmax, t + 1)
                    act.activation(rt[:, 0, :], SA[:, 0:EXPERTS], ACT.Exp, bias=rst[:, 0:1]).then_inc(lexp, 1)

            def iteration(t, centre_on=True, front_on=True, tail_on=True):
                for s in range(2 * STEPS):
                    if s > 0:
                        newton(s // 2, s % 2, t)
                    if s == 1:
                        save_y(t)
                    if tail_on:
                        tail(s, t - 1)
                    if front_on:
                        front(s, t + 1)
                    if s == 0:
                        newton(0, 0, t)
                    if s == 4 and centre_on:
                        squares(t + 2)

            act.wait_ge(zeros_set, 5)
            squares(0)
            for s in range(2 * STEPS):
                front(s, 0)
                if s == 4:
                    squares(1)
            iteration(0, tail_on=False)
            with act.Fori(1, NT - 2) as t:
                iteration(t)
            iteration(NT - 2, centre_on=False)
            iteration(NT - 1, centre_on=False, front_on=False)

            def high_part(c):
                for w, raw in ((wah, w1_a), (wb, w1_b)):
                    act.activation(w[:, c % 3, :], raw[:, c % HID * P:(c % HID + 1) * P], ACT.Copy).then_inc(whi_ready, 1)
            act.wait_ge(ffw_loaded, 64)
            high_part(0)
            high_part(1)
            for s in range(2 * STEPS):
                tail(s, NT - 1)
            with act.Fori(0, NT // GT) as g:
                expert_of = [e for e in range(EXPERTS) for _ in range(WIDTH[e])]
                for c in range(HID):
                    act.wait_ge(up_done, g * HID + c + 1)
                    if c >= 4:
                        act.wait_ge(down_done, g * EXPERTS + expert_of[c - 4] + 1)
                    act.activation(hid[:, c % 4, :], ps[:, c % 2, :], ACT.Gelu_apprx_tanh).then_inc(gelu_done, 1)
                    high_part(c + 2)
                act.wait_ge(down_done, (g + 1) * EXPERTS)

        @block.vector
        def _(dve):
            def centre(t):
                dve.wait_ge(x_loaded, 16 * t + 16)
                dve.tensor_tensor_reduce(out=sq[:], in0=xin, in1=mult, scale=1.0, scalar=0.0, op0=ALU.mult,
                                         op1=ALU.add, accum_out=st[:, 0:1]).then_inc(xmean, 1)
                dve.wait_ge(xmean, t + 1)
                dve.tensor_scalar(st[:, 1:2], st[:, 0:1], 1.0 / FEAT, None, ALU.mult).then_inc(xmean2, 1)
                dve.wait_ge(xmean2, t + 1)
                if later(t):
                    dve.wait_ge(xtr_done, 2 * t)
                    dve.wait_ge(sq_ready, t)
                dve.tensor_scalar(xc.rearrange("p c n -> p (c n)"), xin, st[:, 1:2], None,
                                  ALU.subtract).then_inc(xc_ready, 1)
                dve.wait_ge(xc_ready, t + 1)
                dve.sem_inc(x_free, 1)

            def variance(t):
                dve.wait_ge(sq_ready, t + 1)
                dve.tensor_tensor_reduce(out=sq[:], in0=sq[:], in1=mult, scale=1.0, scalar=0.0, op0=ALU.mult,
                                         op1=ALU.add, accum_out=st[:, 2:3]).then_inc(xvar, 1)

            def less_max(n, t):
                b, h0, nh = ((SA, 0, 8), (SB_, 8, 4))[n]
                dve.wait_ge(smax, 2 * t + 1 + n)
                dve.tensor_tensor(se[:, h0:h0 + nh, :], b[:, 0:nh * 64].rearrange("p (h n) -> p h n", n=64),
                                  sst[:, 0, h0:h0 + nh].unsqueeze(2).to_broadcast([P, nh, 64]),
                                  ALU.subtract).then_inc(sdiff, 1)

            def between(s, t):
                if s == 8:
                    less_max(1, t)
                if s == 11:
                    dve.wait_ge(cst_done, t + 1)
                    dve.tensor_reduce(dmx[:, 0, :], M6[0:HEADS, 0:P].rearrange("p (h n) -> p h n", h=2), AX,
                                      ALU.max).then_inc(dmax, 1)
                    dve.wait_ge(dmax, t + 1)
                    dve.reciprocal(dmx[:, 1, :], dmx[:, 0, :]).then_inc(drec, 1)
                    dve.wait_ge(drec, t + 1)
                    dve.tensor_scalar(dbc[:], dmx[:, 1, :].unsqueeze(2).to_broadcast([HEADS, 2, 64]), -1.0, None,
                                      ALU.mult).then_inc(dbc_ready, 1)

            def front(s, t):
                if s == 1:
                    dve.wait_ge(tok_done, t + 1)
                    dve.wait_ge(xrstd, RSQ * (t + 1))
                    dve.scalar_tensor_tensor(out=h_t[:], in0=M7[:, 0:DIM], scalar=st[:, 4:5], in1=cvec[:],
                                             op0=ALU.mult, op1=ALU.add).then_inc(h_ready, 1)
                    dve.wait_ge(h_ready, t + 1)
                    dve.bn_stats(bn[:, 0:6], h_t[:]).then_inc(bn_a, 1)
                    dve.wait_ge(bn_a, t + 1)
                    dve.tensor_tensor(acc[:, bass.ds(t, 1), :], h_t[:].unsqueeze(1), bp_sb[:].unsqueeze(1),
                                      ALU.add).then_inc(res_saved, 1)
                    dve.bn_aggr(bn[:, 6:8], bn[:, 0:6]).then_inc(bn_b, 1)
                if s == 3:
                    dve.wait_ge(lrstd, LN_RSQ * (t + 1))
                    dve.tensor_scalar(xl[:], h_t[:], bn[:, 6:7], st[:, 5:6], ALU.subtract, ALU.mult).then_inc(xl_ready, 1)
                if s == 5:
                    dve.wait_ge(q_copied, 2 * t + 2)
                if s in (5, 6):
                    for i in (s - 5,):
                        for buf, rows, col, nh, h0 in ((kb_a, P, 2 * P, 8, 0), (kb_b, DB, 3 * P, 4, 8)):
                            dve.tensor_tensor(buf[:, i], M7[0:rows, col + 64 * i:col + 64 * i + 64].unsqueeze(1)
                                              .to_broadcast([rows, nh, 64]),
                                              head_mask[0:rows, h0:h0 + nh].unsqueeze(2).to_broadcast([rows, nh, 64]),
                                              ALU.mult).then_inc(kb_ready, 1)
                if s == 7:
                    dve.wait_ge(scores_done, t + 1)
                    sa = SA.rearrange("p (h n) -> p h n", n=64)
                    sb_ = SB_[:, 0:256].rearrange("p (h n) -> p h n", n=64)
                    dve.tensor_reduce(sst[:, 0, 0:8], sa, AX, ALU.max).then_inc(smax, 1)
                    dve.tensor_reduce(sst[:, 0, 8:12], sb_, AX, ALU.max).then_inc(smax, 1)
                    less_max(0, t)
                if s == 8:
                    dve.wait_ge(probs_exp, t + 1)
                    dve.tensor_reduce(sst[:, 1, :], se[:], AX, ALU.add).then_inc(psumd, 1)
                    dve.wait_ge(psumd, t + 1)
                    dve.reciprocal(sst[:, 2, :], sst[:, 1, :]).then_inc(prec, 1)
                    dve.wait_ge(prec, t + 1)
                    dve.tensor_tensor(se[:], se[:], sst[:, 2, :].unsqueeze(2).to_broadcast([P, HEADS, 64]),
                                      ALU.mult).then_inc(kn_ready, 1)
                if s == 10:
                    dve.wait_ge(kt_done, 2 * t + 2)
                    for n, (b, p0, np_, cs) in enumerate(((TB, 4, 2, colsum_b), (TA, 0, 4, colsum_a))):
                        if n == 1:
                            dve.wait_ge(kt_copied, 4 * t + 2)
                        dve.tensor_reduce(csum[:, p0:p0 + np_, :], b[:, 0:np_ * P].rearrange(
                            "p (h i n) -> p h i n", i=2, n=64), AX, ALU.add).then_inc(cs, 1)

            def front_last(t):
                dve.wait_ge(dbt_done, t + 1)
                dve.tensor_copy(nid[:].rearrange("p h i -> p (h i)"), M7[:, 0:HEADS]).then_inc(nid_ready, 1)
                dve.wait_ge(nid_ready, t + 1)
                for i in range(2):
                    dve.wait_ge(m0_done, 2 * t + i + 1)
                    dve.tensor_tensor(m0[:, i], (SA, SB_)[i][:, 0:PAIRS * ROW].rearrange("p (h c) -> p h c", c=ROW)[:, :, 0:64],
                                      nid[:, :, i:i + 1].to_broadcast([P, PAIRS, 64]), ALU.mult).then_inc(m0_scaled, 1)
                    dve.wait_ge(m0_scaled, 2 * t + i + 1)
                    for half in range(2 - i):
                        a, z = 64 * half, 64 * half + 64
                        dve.tensor_tensor(r0[a:z, i, :, half, :], m0[a:z, i, :, :],
                                          eye[a:z, :].unsqueeze(1).to_broadcast([64, PAIRS, 64]),
                                          ALU.add).then_inc(r0_ready, 1)

            def newton(k, phase, t, images):
                src = r0 if k == 0 else rr
                for i in images:
                    n = 12 * t + 2 * k + i
                    if phase == 0:
                        dve.wait_ge(q_ready, n + 1)
                        for half in range(2):
                            a, z = 64 * half, 64 * half + 64
                            dve.scalar_tensor_tensor(out=uu[a:z, i, :, half, :], in0=src[a:z, i, :, half, :], scalar=3.0,
                                                     in1=qq[a:z, i], op0=ALU.mult, op1=ALU.add).then_inc(u_ready, 1)
                    elif k == STEPS - 1:
                        dve.wait_ge(prod_done, n + 1)
                        for half in range(2):
                            a, z = 64 * half, 64 * half + 64
                            dve.scalar_tensor_tensor(out=rr[a:z, i, :, half, :], in0=NB[i][a:z], scalar=-0.25,
                                                     in1=eye[a:z, :].unsqueeze(1).to_broadcast([64, PAIRS, 64]),
                                                     op0=ALU.mult, op1=ALU.add).then_inc(r_ready, 1)

            def tail(s, t):
                if s == 1:
                    dve.wait_ge(proj_done, t + 1)
                    dve.wait_ge(res_saved, t + 1)
                    if later(t):
                        dve.wait_ge(h2_saved, t)
                    dve.tensor_tensor(h2[:].unsqueeze(1), M6[:, 0:DIM].unsqueeze(1), acc[:, bass.ds(t, 1), :],
                                      ALU.add).then_inc(h2_ready, 1)
                    dve.wait_ge(h2_ready, t + 1)
                    dve.bn_stats(bn2[:, 0:6], h2[:]).then_inc(tbn_a, 1)
                    wait_first(tbn_a, t + 1)
                    dve.bn_aggr(bn2[:, 6:8], bn2[:, 0:6]).then_inc(tbn_b, 1)
                if s == 3:
                    dve.wait_ge(trstd, LN_RSQ * (t + 1))
                    dve.tensor_scalar(x2[:, 0:DIM], h2[:], bn2[:, 6:7], rst[:, 1:2], ALU.subtract,
                                      ALU.mult).then_inc(x2_ready, 1)
                    dve.tensor_scalar(x2[:, DIM:], h2[:, DA:], bn2[:, 6:7], rst[:, 1:2], ALU.subtract,
                                      ALU.mult).then_inc(x2_ready, 1)
                if s == 5:
                    dve.wait_ge(logits_done, t + 1)
                    dve.tensor_reduce(rst[:, 0:1], SA[:, 0:EXPERTS], AX, ALU.max, negate=True).then_inc(lmax, 1)
                if s == 7:
                    wait_first(lexp, t + 1)
                    dve.max(rt[:, 1, 0:TOPK], rt[:, 0, :]).then_inc(ltop, 1)
                    wait_first(ltop, t + 1)
                    dve.match_replace(rt[:, 2, :], rt[:, 1, 0:TOPK], rt[:, 0, :], -1.0).then_inc(lrep, 1)
                    dve.wait_ge(lrep, t + 1)
                    dve.scalar_tensor_tensor(out=rt[:, 3, :], in0=rt[:, 2, :], scalar=0.0, in1=rt[:, 0, :],
                                             op0=ALU.is_lt, op1=ALU.mult).then_inc(lsel, 1)
                    dve.wait_ge(lsel, t + 1)
                    dve.tensor_reduce(rst[:, 2:3], rt[:, 3, :], AX, ALU.add).then_inc(lsum, 1)
                    dve.wait_ge(lsum, t + 1)
                    dve.reciprocal(rst[:, 3:4], rst[:, 2:3]).then_inc(linv, 1)
                    dve.wait_ge(linv, t + 1)
                    dve.tensor_scalar(comb[:, bass.ds(t, 1), :], rt[:, 3, :].unsqueeze(1), rst[:, 3:4], None,
                                      ALU.mult).then_inc(comb_ready, 1)

            def iteration(t, centre_on=True, front_on=True, tail_on=True):
                for s in range(2 * STEPS):
                    newton(s // 2, s % 2, t, (0,))
                    if front_on:
                        between(s, t + 1)
                    newton(s // 2, s % 2, t, (1,))
                    if s == 5 and centre_on:
                        variance(t + 2)
                    if tail_on:
                        tail(s, t - 1)
                    if front_on:
                        front(s, t + 1)
                    if s == 2 and centre_on:
                        centre(t + 2)
                if front_on:
                    front_last(t + 1)

            dve.memset(scrap[:], 0.0).then_inc(scrap_set, 1)
            dve.wait_ge(scrap_set, 1)
            dve.wait_ge(const_loaded, 16)
            centre(0)
            variance(0)
            n = 0
            for hh in range(2):
                if hh == 0:
                    dve.wait_ge(wsh_top_loaded, 32)
                else:
                    dve.wait_ge(wsh_loaded, 48)
                for f in range(5):
                    for ch in range(3):
                        c = 3 * hh + ch
                        g = gbs[:, 0, hh * 15 + 3 * f + ch:hh * 15 + 3 * f + ch + 1]
                        if f == 0:
                            dve.tensor_scalar(weff[:, c, :], wsh[:, hh, f, ch, :], g, None, ALU.mult).then_inc(folded, 1)
                        else:
                            dve.wait_ge(folded, n - 2)
                            dve.scalar_tensor_tensor(out=weff[:, c, :], in0=wsh[:, hh, f, ch, :], scalar=g,
                                                     in1=weff[:, c, :], op0=ALU.mult, op1=ALU.add).then_inc(folded, 1)
                        n += 1
            for c in range(2):
                dve.tensor_scalar(weff[:, 6 + c, :], whalo[:, c, :], gbs[:, 0, 30 + c:31 + c], None,
                                  ALU.mult).then_inc(folded, 1)
            dve.wait_ge(beta_done, 1)
            dve.tensor_copy(crow[:], M6[0:1, 0:DIM]).then_inc(crow_ready, 1)
            dve.wait_ge(cbc_done, 1)
            dve.tensor_tensor(cvec[:], M7[:, 0:DIM], tokb[:], ALU.add).then_inc(cvec_ready, 1)
            dve.wait_ge(cvec_ready, 1)
            for s in range(2 * STEPS):
                between(s, 0)
                front(s, 0)
                if s == 2:
                    centre(1)
                if s == 4:
                    variance(1)
            front_last(0)
            iteration(0, tail_on=False)
            with dve.Fori(1, NT - 2) as t:
                iteration(t)
            iteration(NT - 2, centre_on=False)
            iteration(NT - 1, centre_on=False, front_on=False)

            def low_part(g, c):
                dve.wait_ge(whi_ready, (g * HID + c + 1) * 2)
                k, col = c % 3, c % HID * P
                for w, high, raw, a in ((wal, wah, w1_a, 0), (wb, wb, w1_b, 64)):
                    dve.tensor_tensor(w[a:P, k, :], raw[a:P, col:col + P], high[a:P, k, :].bitcast(F32),
                                      ALU.subtract).then_inc(wlo_ready, 1)
            dve.wait_ge(ffw_loaded, 64)
            low_part(0, 0)
            low_part(0, 1)
            for s in range(2 * STEPS):
                tail(s, NT - 1)

            dve.wait_ge(comb_ready, NT)
            dve.wait_ge(h2_saved, NT)
            dve.tensor_copy(scrap[:, 0:1], scrap[:, 1:2]).then_inc(expert_added, 1)
            dve.tensor_copy(scrap[:, 2:3], scrap[:, 1:2]).then_inc(expert_added, 1)
            with dve.Fori(0, NT // GT) as g:
                c = 0
                for e in range(EXPERTS):
                    for _ in range(WIDTH[e]):
                        low_part(g, c + 2)
                        c += 1
                    dve.wait_ge(down_done, g * EXPERTS + e + 1)
                    dve.wait_ge(expert_added, g * EXPERTS + e + 2)
                    for j in range(GT):
                        a = acc[:, bass.ds(g * GT + j, 1), :]
                        last = dve.scalar_tensor_tensor(
                            out=a, in0=ps[:, 2 + 2 * (e % 2) + j // 2, (j % 2) * DIM:(j % 2 + 1) * DIM].unsqueeze(1),
                            scalar=comb[:, bass.ds(g * GT + j, 1), e:e + 1].rearrange("p a b -> p (a b)"), in1=a,
                            op0=ALU.mult, op1=ALU.add)
                    last.then_inc(expert_added, 1)


def kernel(x, L0_tok_gamma, L0_tok_beta, L0_tok_W, L0_tok_b, L0_attn_w_qkv, L0_attn_w_proj, L0_attn_b_proj,
           L0_ffn_router_w, L0_ffn_w1, L0_ffn_w2):
    import numpy as np
    import concourse.bacc as bacc
    from concourse.bass_utils import run_bass_kernel_spmd

    x = np.asarray(x)
    pad = np.zeros((IMGS, 130, 130, 3), x.dtype)
    pad[:, 1:129, 1:129] = x
    def rows_of(a, first):
        return a[:, first:first + 113:16]
    inner = np.ascontiguousarray(pad[:, 1:129, 1:129]).reshape(IMGS, 8, 2, 8, 8, 16, 3)
    inner = inner.transpose(0, 1, 4, 2, 6, 3, 5).reshape(IMGS * TOK, 768)
    side = np.stack([pad[:, 1:129, 0:113:16], pad[:, 1:129, 17:130:16]], 3)
    side = side.reshape(IMGS, 8, 16, 8, 2, 3).transpose(0, 1, 3, 2, 4, 5).reshape(IMGS * TOK, 96)
    ends = np.stack([rows_of(pad, 0), rows_of(pad, 17)], 2)[:, :, :, 1:129]
    ends = ends.reshape(IMGS, 8, 2, 8, 16, 3).transpose(0, 1, 3, 2, 4, 5).reshape(IMGS * TOK, 96)
    gap = np.zeros((IMGS * TOK, 32), x.dtype)
    xw = np.concatenate([inner, side, gap, ends, gap], 1).reshape(NT, P, CH * P)

    def by_pixel(a):
        a = np.asarray(a).reshape(16, 16, 5, 3, -1)
        z = np.zeros_like(a)
        z[:, :, 0] = a[:, :, 0]
        z[:, :15, 1] = a[:, 1:, 1]
        z[:, 1:, 2] = a[:, :15, 2]
        z[:15, :, 3] = a[1:, :, 3]
        z[1:, :, 4] = a[:15, :, 4]
        inside = z.reshape(2, P, 5, 3, -1).transpose(1, 0, 2, 3, 4)
        border = np.zeros((P, 2, a.shape[-1]), a.dtype)
        border[:96, 0] = np.stack([a[:, 0, 1], a[:, 15, 2]], 1).reshape(96, -1)
        border[:96, 1] = np.stack([a[0, :, 3], a[15, :, 4]], 0).reshape(96, -1)
        return inside, border

    wsh, whalo = by_pixel(L0_tok_W)
    gs, gh = by_pixel(L0_tok_gamma)
    bs, bh = by_pixel(L0_tok_beta)
    gb = np.stack([np.concatenate([gs.reshape(P, 30), gh[:, :, 0]], 1),
                   np.concatenate([bs.reshape(P, 30), bh[:, :, 0]], 1)], 1)

    wt = np.asarray(L0_attn_w_qkv).T
    wqk = wt[:, :2 * DIM]
    wv = wt[:, 2 * DIM:].reshape(DIM, PAIRS, 2, HD).transpose(0, 2, 1, 3).reshape(DIM, DIM)
    pt = np.asarray(L0_attn_w_proj).T.reshape(PAIRS, 2, HD, DIM)
    wp = np.zeros((4, 32, 4, DIM), pt.dtype)
    for p in range(PAIRS):
        for half in range(2):
            wp[p % 4, :HD, 2 * (p // 4) + half] = pt[p, half]

    const = np.zeros((P, C_ALL), np.float32)
    const[:, C_ID:C_ID + P] = np.eye(P)
    const[:, C_EYE:C_EYE + 64] = np.tile(np.eye(64), (2, 1))
    for p in range(P):
        const[p, C_HM + p // HD] = 1
        if p < DB:
            const[p, C_HM + 8 + p // HD] = 1
    const[:, C_PC:C_PC + 8] = [1 / FEAT, 1e-3, 1, 1e-5, -0.5, 1.5, 0, 0]
    copies = np.ones((16, 16), np.float32)
    copies[:, :15] += 1
    copies[:, 1:] += 1
    copies[:15] += 1
    copies[1:] += 1
    const[:, C_MULT:C_MULT + 768] = np.repeat(copies.reshape(2, 1, P), 3, 1).reshape(-1)
    const[:, C_MULT + 768:C_MULT + 864] = 1
    const[:, C_MULT + 896:C_MULT + 992] = 1

    arrays = {
        "x_dram": xw, "ws_dram": wsh, "wh_dram": whalo, "gb_dram": gb, "tb_dram": L0_tok_b,
        "wqk_dram": wqk, "wv_dram": wv, "wp_dram": wp.reshape(P, 4, DIM), "bp_dram": L0_attn_b_proj,
        "rw_dram": np.asarray(L0_ffn_router_w).T, "w1_dram": L0_ffn_w1, "w2_dram": L0_ffn_w2, "const_dram": const,
    }
    arrays = {k: np.ascontiguousarray(v) for k, v in arrays.items()}
    nc = bacc.Bacc("TRN2", target_bir_lowering=False, num_devices=1)
    args = [nc.dram_tensor(k, v.shape, mybir.dt.from_np(v.dtype), kind="ExternalInput").ap() for k, v in arrays.items()]
    args.append(nc.dram_tensor("out_dram", (NT, P, DIM), F32, kind="ExternalOutput").ap())
    vit_block_kernel(nc, *args)
    r = run_bass_kernel_spmd(nc, [arrays], core_ids=[0])
    return np.asarray(r.results[0]["out_dram"]).reshape(IMGS, TOK, DIM)
```
